# Optimizing a Trainium2 kernel written in Bass

```python
import numpy as np
import jax
import jax.numpy as jnp

def _softmax(x, axis=-1):
    return jax.nn.softmax(x, axis=axis)

def _gelu(x):
    return jax.nn.gelu(x, approximate=True)

def _silu(x):
    return jax.nn.silu(x)

def _sigmoid(x):
    return jax.nn.sigmoid(x)

def _layernorm(x, axis=-1, eps=1e-05):
    m = jnp.mean(x, axis=axis, keepdims=True)
    v = jnp.var(x, axis=axis, keepdims=True)
    return (x - m) / jnp.sqrt(v + eps)

def _scatter_add(tgt, idx, src, axis=0):
    return tgt.at[idx].add(src)

def _segment_sum(src, seg, n):
    return jax.ops.segment_sum(src, seg, n)
kernel_name = 'mk_xattn_ffn_d1_seqx_r2_7045af'

def setup_inputs(seed: int=0):
    np.random.seed(seed)
    _w = jnp.asarray

    def _rec_inputs():
        import jax
        import jax.numpy as jnp
        _rk = jax.random.key(seed)
        x = -0.0003929 + 0.9999 * jax.random.normal(jax.random.fold_in(_rk, 1), (4, 2048, 512), jnp.float32)
        _lenS = 2048 - jax.random.randint(jax.random.fold_in(_rk, 7), (4,), 0, max(1, 2048 // 4) + 1, jnp.int32)
        _lenS2 = 154 - jax.random.randint(jax.random.fold_in(_rk, 8), (4,), 0, max(1, 154 // 4) + 1, jnp.int32)
        _ctx_1024P = jax.random.normal(jax.random.fold_in(_rk, 11), (4, 16, 512), jnp.float32)
        _ctx_1024c = jax.random.dirichlet(jax.random.fold_in(_rk, 511), 0.3 * jnp.ones((16,), jnp.float32), (4, 154))
        _ctx_1024t = jnp.einsum('bsk,bkd->bsd', _ctx_1024c, _ctx_1024P)
        _ctx_1024t = _ctx_1024t * jax.lax.rsqrt(jnp.mean(jnp.square(_ctx_1024t)) + 1e-12) * 0.953939
        ctx_1024 = -0.000514642 + 1.00011 * (_ctx_1024t + 0.3 * jax.random.normal(jax.random.fold_in(_rk, 611), (4, 154, 512), jnp.float32))
        itok_BxS_0_511 = jax.random.randint(jax.random.fold_in(_rk, 12), (4, 2048), 0, 256, jnp.int32)
        return (x, ctx_1024, itok_BxS_0_511)
    x, ctx_1024, itok_BxS_0_511 = _rec_inputs()

    def _L0_xattn_setup():
        import jax, jax.numpy as jnp
        import numpy as np
        Q_DIM = 512
        KV_DIM = 512
        D_ATTN = 512
        N_HEADS = 16
        HDIM = D_ATTN // N_HEADS
        LOOKBACK = 3
        KW = LOOKBACK + 1
        SCALE = HDIM ** (-0.5)
        B, LQ, LKV = (4, 2048, 256)

        def _split_heads(x):
            b, l, _ = x.shape
            return x.reshape(b, l, N_HEADS, HDIM).transpose(0, 2, 1, 3)
        key = jax.random.key(seed)
        ks = jax.random.split(key, 6)
        q = jax.random.normal(ks[0], (B, LQ, Q_DIM), dtype=jnp.float32)
        kv_src = jax.random.normal(ks[1], (B, LKV, KV_DIM), dtype=jnp.float32)
        seg_id = jnp.sort(jax.random.randint(ks[2], (B, LQ), 0, LKV), axis=-1)
        Wq = jax.random.normal(ks[3], (D_ATTN, Q_DIM), dtype=jnp.float32) * Q_DIM ** (-0.5)
        Wkv = jax.random.normal(ks[4], (2 * D_ATTN, KV_DIM), dtype=jnp.float32) * KV_DIM ** (-0.5)
        Wo = jax.random.normal(ks[5], (Q_DIM, D_ATTN), dtype=jnp.float32) * D_ATTN ** (-0.5)
        return {'q': q, 'kv_src': kv_src, 'seg_id': seg_id, 'Wq': Wq, 'Wkv': Wkv, 'Wo': Wo}
    _L0_xattn_all = _L0_xattn_setup()
    _L0_xattn_in = {k: v for k, v in _L0_xattn_all.items() if k in ('Wq', 'Wkv', 'Wo')}
    del _L0_xattn_all

    def _L0_ffn_setup():
        import jax, jax.numpy as jnp
        import numpy as np
        BLOCK = 32
        W_BITS = 4
        ACT_BITS = 16

        def act_qdq(x):
            qmax = 2.0 ** (ACT_BITS - 1) - 1.0
            scale = jnp.maximum(jnp.max(jnp.abs(x)) / qmax, 1e-12)
            return jnp.clip(jnp.round(x / scale), -qmax - 1.0, qmax) * scale

        def fixed_qdq_u16(x):
            scale = 1.0 / 65536.0
            return jnp.clip(jnp.round(x / scale), 0.0, 65535.0) * scale

        def lpbq_dequant(w):
            O, I = w.shape
            qmax = 2.0 ** (W_BITS - 1) - 1.0
            wb = w.reshape(O, I // BLOCK, BLOCK)
            s = jnp.maximum(jnp.max(jnp.abs(wb), axis=-1, keepdims=True) / qmax, 1e-12)
            wq = jnp.clip(jnp.round(wb / s), -qmax - 1.0, qmax) * s
            return wq.reshape(O, I)
        key = jax.random.key(seed)
        k1, k2, k3, k4 = jax.random.split(key, 4)
        B, S, H, I = (2, 2048, 512, 1536)
        x = jax.random.normal(k1, (B, S, H), jnp.float32)
        w_gate = jax.random.normal(k2, (I, H), jnp.float32) * 0.02
        w_up = jax.random.normal(k3, (I, H), jnp.float32) * 0.02
        w_down = jax.random.normal(k4, (H, I), jnp.float32) * 0.02
        return {'x': x, 'w_gate': w_gate, 'w_up': w_up, 'w_down': w_down}
    _L0_ffn_all = _L0_ffn_setup()
    _L0_ffn_in = {k: v for k, v in _L0_ffn_all.items() if k in ('w_gate', 'w_up', 'w_down')}
    del _L0_ffn_all
    return {'x': x, 'ctx_1024': ctx_1024, 'itok_BxS_0_511': itok_BxS_0_511, 'L0_xattn_Wq': _L0_xattn_in['Wq'], 'L0_xattn_Wkv': _L0_xattn_in['Wkv'], 'L0_xattn_Wo': _L0_xattn_in['Wo'], 'L0_ffn_w_gate': _L0_ffn_in['w_gate'], 'L0_ffn_w_up': _L0_ffn_in['w_up'], 'L0_ffn_w_down': _L0_ffn_in['w_down']}

def reference(x, ctx_1024, itok_BxS_0_511, L0_xattn_Wq, L0_xattn_Wkv, L0_xattn_Wo, L0_ffn_w_gate, L0_ffn_w_up, L0_ffn_w_down):
    import jax
    import jax.numpy as jnp

    def _L0_xattn_ref(q, kv_src, seg_id, Wq, Wkv, Wo):
        import jax, jax.numpy as jnp
        import numpy as np
        Q_DIM = 512
        KV_DIM = 512
        D_ATTN = 512
        N_HEADS = 16
        HDIM = D_ATTN // N_HEADS
        LOOKBACK = 3
        KW = LOOKBACK + 1
        SCALE = HDIM ** (-0.5)
        B, LQ, LKV = (4, 2048, 256)

        def _split_heads(x):
            b, l, _ = x.shape
            return x.reshape(b, l, N_HEADS, HDIM).transpose(0, 2, 1, 3)
        b, lq, _ = q.shape
        lkv = kv_src.shape[1]
        qh = _split_heads(q @ Wq.T)
        kv = kv_src @ Wkv.T
        k, v = jnp.split(kv, 2, axis=-1)
        kh = _split_heads(k)
        vh = _split_heads(v)
        offsets = jnp.arange(KW)
        gather = seg_id[:, :, None] - offsets
        neg_mask = gather < 0
        gc = jnp.clip(gather, 0, lkv - 1)
        b_idx = jnp.arange(b)[:, None, None]
        k_sel = kh[b_idx, :, gc].transpose(0, 3, 1, 2, 4)
        v_sel = vh[b_idx, :, gc].transpose(0, 3, 1, 2, 4)
        scores = jnp.einsum('bhqd,bhqkd->bhqk', qh, k_sel) * SCALE
        neg_inf = jnp.finfo(scores.dtype).min
        scores = jnp.where(neg_mask[:, None, :, :], neg_inf, scores)
        probs = jax.nn.softmax(scores, axis=-1)
        out = jnp.einsum('bhqk,bhqkd->bhqd', probs, v_sel)
        out = out.transpose(0, 2, 1, 3).reshape(b, lq, D_ATTN)
        return out @ Wo.T

    def _L0_ffn_ref(x, w_gate, w_up, w_down):
        import jax, jax.numpy as jnp
        import numpy as np
        BLOCK = 32
        W_BITS = 4
        ACT_BITS = 16

        def act_qdq(x):
            qmax = 2.0 ** (ACT_BITS - 1) - 1.0
            scale = jnp.maximum(jnp.max(jnp.abs(x)) / qmax, 1e-12)
            return jnp.clip(jnp.round(x / scale), -qmax - 1.0, qmax) * scale

        def fixed_qdq_u16(x):
            scale = 1.0 / 65536.0
            return jnp.clip(jnp.round(x / scale), 0.0, 65535.0) * scale

        def lpbq_dequant(w):
            O, I = w.shape
            qmax = 2.0 ** (W_BITS - 1) - 1.0
            wb = w.reshape(O, I // BLOCK, BLOCK)
            s = jnp.maximum(jnp.max(jnp.abs(wb), axis=-1, keepdims=True) / qmax, 1e-12)
            wq = jnp.clip(jnp.round(wb / s), -qmax - 1.0, qmax) * s
            return wq.reshape(O, I)
        x = act_qdq(x)
        up = act_qdq(x @ lpbq_dequant(w_up).T)
        gate = act_qdq(x @ lpbq_dequant(w_gate).T)
        sig = fixed_qdq_u16(jax.nn.sigmoid(gate))
        gate = act_qdq(gate * sig)
        o = act_qdq(gate * up)
        return o @ lpbq_dequant(w_down).T
    x = x + _L0_xattn_ref(_layernorm(x, axis=-1), ctx_1024, itok_BxS_0_511, L0_xattn_Wq, L0_xattn_Wkv, L0_xattn_Wo)
    x = x + _L0_ffn_ref(_layernorm(x, axis=-1), L0_ffn_w_gate, L0_ffn_w_up, L0_ffn_w_down)
    return x

_drawn_inputs = setup_inputs


def setup_inputs(seed=0):
    import zlib

    import numpy as np

    out = dict(_drawn_inputs(seed))
    spreads = {}
    factors = {}
    for name, (base, spread) in spreads.items():
        noise = np.random.default_rng([zlib.crc32(name.encode()), seed]).standard_normal(out[name].shape)
        drawn = base * np.exp(spread * noise) if base else spread * noise
        out[name] = jnp.asarray(drawn.astype(out[name].dtype))
    for name, factor in factors.items():
        out[name] = (out[name] * factor).astype(out[name].dtype)
    return out
```

```python
from contextlib import ExitStack

import concourse.bass as bass
from concourse import mybir

F32 = mybir.dt.float32
F16 = mybir.dt.float16
I16 = mybir.dt.int16
U16 = mybir.dt.uint16
I32 = mybir.dt.int32
ALU = mybir.AluOpType
ACT = mybir.ActivationFunctionType
AX = mybir.AxisListType
PEAK = bass.bass_isa.ReduceOp.max

P = 128
D = 512
DC = D // P
H, HD = 16, 32
W = 4
F = 1536
FC = F // P
QB = 32
BLK = 512
SUB = BLK // P
EPS = 1e-5
QMAX = 32767.0
WMAX = 7.0
TINY = 1e-12
SPAN = 1024.0
VSPAN = 64.0
LOW = -3.0e38
UN = 4
UNITS = FC // UN
UE = UN * BLK


def need(eng, sem, value):
    if isinstance(value, int) and value <= 0:
        return
    eng.wait_ge(sem, value)


class Tick:

    def __init__(self, n, unroll, u, k=None, s=None):
        self.n, self.unroll, self.u, self.k, self.s = n, unroll, u, k, s

    def at(self, off=0):
        return self.div(off, 1)

    def div(self, off, m, per=1, add=0):
        if self.k is None:
            return ((self.s + off) * per + add) // m
        assert self.unroll * per % m == 0
        return self.k * (self.unroll * per // m) + ((self.u + off) * per + add) // m

    def live(self, off=0):
        return self.k is not None or 0 <= self.s + off < self.n

    def live_unit(self, per, add):
        return self.k is not None or 0 <= self.s * per + add < self.n * per


def pipeline(eng, tick, n, unroll, before=0, after=0):
    assert n % unroll == 0 and n // unroll >= 3 and before <= unroll and after <= unroll
    for s in range(-before, unroll):
        tick(Tick(n, unroll, s % unroll, s=s))
    with eng.Fori(1, n // unroll - 1) as k:
        for u in range(unroll):
            tick(Tick(n, unroll, u, k=k))
    for s in range(n - unroll, n + after):
        tick(Tick(n, unroll, s % unroll, s=s))


class Transfers:

    def __init__(self, scope, name, slots, each=16):
        self.sems, self.slots, self.each = [scope.sem(f"{name}{i}") for i in range(slots)], slots, each

    def of(self, c, off=0, per=1, add=0):
        return self.sems[((c.u + off) * per + add) % self.slots]

    def done(self, eng, c, off=0, per=1, add=0):
        need(eng, self.of(c, off, per, add), self.each * (c.div(off, self.slots, per, add) + 1))

    def all_done(self, eng, n):
        for i, sem in enumerate(self.sems):
            need(eng, sem, self.each * ((n - i + self.slots - 1) // self.slots))


class Scope:

    def __init__(self, nc, tag):
        self.nc, self.tag, self.ctx, self.own = nc, tag, ExitStack(), []

    def __enter__(self):
        self.ctx.__enter__()
        return self

    def __exit__(self, *a):
        if self.own and a[0] is None:
            self.nc.clear_and_free_semaphores(self.own)
            self.nc.all_engine_barrier()
        return self.ctx.__exit__(*a)

    def sb(self, name, shape, dt):
        return self.ctx.enter_context(self.nc.sbuf_tensor(f"{self.tag}_{name}", shape, dt))

    def ps(self, name, shape, dt=F32):
        return self.ctx.enter_context(self.nc.psum_tensor(f"{self.tag}_{name}", shape, dt))

    def sem(self, name):
        self.own.append(self.nc.alloc_semaphore(f"{self.tag}_{name}"))
        return self.own[-1]

    def sems(self, names):
        return {n: self.sem(n) for n in names.split()}


def chain(eng, sem):
    count = [0]

    def link(ins):
        count[0] += 1
        ins.then_inc(sem, 1)
        eng.wait_ge(sem, count[0])
    return link


def prepare_dense(nc, keep, x, ctx_t, idx_t, wq_t, wkv_t, wo_t, table, B, LKV):
    T = x.shape[0]
    NT = T // P
    PER = NT // B
    ROWS = LKV + 6
    TAIL = LKV - P
    XG = 2
    with Scope(nc, "pd") as s:
        fq, fo = s.sb("fq", [P, DC * D], F32), s.sb("fo", [P, DC * D], F32)
        fkv, fc = s.sb("fkv", [P, DC * 2 * D], F32), s.sb("fc", [P, DC * B * LKV], F32)
        kv_w = [s.sb(f"kv_w{i}", [P, DC, 2 * D], F16) for i in range(2)]
        cx = [s.sb(f"cx{i}", [P, DC, B, LKV], F16) for i in range(2)]
        kv = s.sb("kv", [P, 2 * B, 2 * D], F32)
        xg = s.sb("xg", [P, 2, XG, D], F32)
        peaks, allp, unit = s.sb("peaks", [P, 4], F32), s.sb("allp", [P, 4], F32), s.sb("unit", [P, 4], F32)
        vcol, vred, vall, vinv = (s.sb(n, [P, m], F32) for n, m in (("vcol", 2 * B), ("vred", 1), ("vall", 1), ("vinv", 1)))
        stats, mv = s.sb("stats", [P, NT, 6], F32), s.sb("mv", [P, NT, 2], F32)
        veps, lnv, y0, y1, y2 = (s.sb(n, [P, NT], F32) for n in ("veps", "lnv", "y0", "y1", "y2"))
        ids, idf = s.sb("ids", [P, NT], I32), s.sb("idf", [P, NT], F32)
        pk = [s.ps(f"pk{i}", [P, D]) for i in range(8)]
        m = s.sems("ids peaks all unit split_hi split_lo kv_ready k_out v_out v_peak v_all v_scaled "
                         "stat ln dve rows_out veps")
        loads = [(fq, wq_t, keep["wq"]), (fo, wo_t, keep["wo"]), (fkv, wkv_t, None), (fc, ctx_t, None)]
        x_loaded = [s.sem(f"x_loaded{i}") for i in range(2)]
        mat_in = [s.sem(f"mat_in{i}") for i in range(4)]
        pairs = [(keep["wq"], fq), (keep["wo"], fo), (kv_w, fkv), (cx, fc)]

        def flat(t):
            return t.rearrange("p a b c -> p (a b c)") if len(t.shape) == 4 else t.rearrange("p a b -> p (a b)")

        with nc.Block() as block:
            @block.sync
            def _(sp):
                sp.dma_start(ids[:, :], idx_t).then_inc(m["ids"], 16)
                for i in (3, 2, 0, 1):
                    sp.dma_start(loads[i][0][:, :], loads[i][1]).then_inc(mat_in[i], 16)
                for g in range(NT // XG):
                    need(sp, m["stat"], (g - 1) * XG)
                    sp.dma_start(xg[:, g % 2], x[g * XG * P:(g + 1) * XG * P, :].rearrange(
                        "(n p) d -> p n d", p=P)).then_inc(x_loaded[g % 2], 16)
                sp.wait_ge(m["v_scaled"], 1)
                for b in range(B):
                    lo, hi = kv[:, 2 * b, :], kv[:, 2 * b + 1, :]
                    sp.dma_start(table[b * ROWS + 3:b * ROWS + 3 + P, :], lo).then_inc(m["rows_out"], 16)
                    sp.dma_start(table[b * ROWS + 3 + P:b * ROWS + 3 + LKV, :], hi[0:TAIL]).then_inc(m["rows_out"], 16)
                    for j in range(3):
                        sp.dma_start(table[b * ROWS + j:b * ROWS + j + 1, :], lo[0:1]).then_inc(m["rows_out"], 16)
                        sp.dma_start(table[b * ROWS + 3 + LKV + j:b * ROWS + 4 + LKV + j, :],
                                     hi[TAIL - 1:TAIL]).then_inc(m["rows_out"], 16)
                sp.wait_ge(m["rows_out"], 16 * 8 * B)

            @block.vector
            def _(dve):
                link = chain(dve, m["dve"])
                for i, (f, _, _) in enumerate(loads):
                    dve.wait_ge(mat_in[i], 16)
                    last = nc.vector.tensor_reduce(peaks[:, i:i + 1], f[:, :], AX.X, ALU.max, apply_absolute_value=True)
                last.then_inc(m["peaks"], 1)
                link(nc.vector.memset(vcol[:, :], 0.0))
                dve.wait_ge(m["ids"], 16)
                link(nc.vector.tensor_scalar(idf[:, :], ids[:, :], 0.0, float(LKV + 2), ALU.max, ALU.min))
                for j in range(W):
                    nc.vector.tensor_scalar(keep["mask"][:, :, j], idf[:, :], float(3 - j), LOW, ALU.is_lt, ALU.mult)
                for b in range(B):
                    link(nc.vector.tensor_scalar(keep["rows"][:, b * PER:(b + 1) * PER], idf[:, b * PER:(b + 1) * PER],
                                                 float(b * ROWS), None, ALU.add))
                dve.wait_ge(m["all"], 1)
                link(nc.vector.tensor_scalar(keep["alpha"][:, 0:4], allp[:, :], 1e-30, 1.0 / SPAN, ALU.max, ALU.mult))
                nc.vector.reciprocal(unit[:, :], keep["alpha"][:, 0:4]).then_inc(m["unit"], 1)
                dve.wait_ge(m["unit"], 1)
                for n, i in enumerate((3, 2, 0, 1)):
                    (hi, lo), f = pairs[i]
                    link(nc.vector.tensor_scalar(f[:, :], f[:, :], unit[:, i:i + 1], None, ALU.mult))
                    link(nc.vector.tensor_copy(flat(hi[:]), f[:, :]))
                    nc.vector.tensor_tensor(flat(lo[:]), f[:, :], flat(hi[:]), ALU.subtract).then_inc(m["split_lo"], 1)
                for t in range(NT):
                    if t % XG == 0:
                        dve.wait_ge(x_loaded[t // XG % 2], 16 * (t // XG // 2 + 1))
                    nc.vector.bn_stats(stats[:, t, :], xg[:, t // XG % 2, t % XG, :]).then_inc(m["stat"], 1)
                    if t == XG:
                        dve.wait_ge(m["v_out"], 2 * B)
                        for i in range(2 * B):
                            rows = P if i % 2 == 0 else TAIL
                            last = nc.vector.tensor_reduce(vcol[0:rows, i:i + 1], kv[0:rows, i, D:2 * D], AX.X, ALU.max,
                                                           apply_absolute_value=True)
                        link(last)
                        nc.vector.tensor_reduce(vred[:, :], vcol[:, :], AX.X, ALU.max).then_inc(m["v_peak"], 1)
                dve.wait_ge(m["stat"], NT)
                for t in range(NT):
                    last = nc.vector.bn_aggr(mv[:, t, :], stats[:, t, :])
                link(last)
                nc.vector.tensor_scalar(veps[:, :], mv[:, :, 1], EPS, None, ALU.add).then_inc(m["veps"], 1)
                dve.wait_ge(m["v_all"], 1)
                link(nc.vector.tensor_scalar(vinv[:, :], vall[:, :], 1e-30, 1.0 / VSPAN, ALU.max, ALU.mult))
                nc.vector.tensor_copy(keep["alpha"][:, 7:8], vinv[:, :])
                link(nc.vector.reciprocal(unit[:, 0:1], vinv[:, :]))
                dve.wait_ge(m["k_out"], 2 * B)
                for i in range(2 * B):
                    rows = P if i % 2 == 0 else TAIL
                    last = nc.vector.tensor_scalar(kv[0:rows, i, D:2 * D], kv[0:rows, i, D:2 * D], unit[0:rows, 0:1], None, ALU.mult)
                last.then_inc(m["v_scaled"], 1)
                dve.wait_ge(m["ln"], 2)
                link(nc.vector.tensor_tensor(y1[:, :], y0[:, :], y0[:, :], ALU.mult))
                link(nc.vector.tensor_tensor(y2[:, :], y1[:, :], veps[:, :], ALU.mult))
                link(nc.vector.tensor_scalar(y1[:, :], y2[:, :], -0.5, 1.5, ALU.mult, ALU.add))
                link(nc.vector.tensor_tensor(keep["rstd"][:, :], y0[:, :], y1[:, :], ALU.mult))
                link(nc.vector.scalar_tensor_tensor(out=keep["shift"][:, :], in0=mv[:, :, 0], scalar=-1.0,
                                                    in1=keep["rstd"][:, :], op0=ALU.mult, op1=ALU.mult))
                al = keep["alpha"]
                link(nc.vector.tensor_tensor(al[:, 8:9], al[:, 2:3], al[:, 3:4], ALU.mult))
                link(nc.vector.tensor_scalar(al[:, 9:10], al[:, 8:9], al[:, 0:1], float(HD) ** -0.5, ALU.mult, ALU.mult))
                link(nc.vector.tensor_scalar(al[:, 10:11], al[:, 8:9], al[:, 1:2], al[:, 7:8], ALU.mult, ALU.mult))

            @block.scalar
            def _(act):
                for i in range(2 * B):
                    rows = P if i % 2 == 0 else TAIL
                    for half in range(2):
                        n = 2 * i + half
                        act.wait_ge(m["kv_ready"], n + 1)
                        nc.scalar.activation(kv[0:rows, i, half * D:(half + 1) * D], pk[n % 8][0:rows, :],
                                             ACT.Copy).then_inc(m["v_out" if half else "k_out"], 1)
                act.wait_ge(m["veps"], 1)
                nc.scalar.activation(lnv[:, :], veps[:, :], ACT.Ln).then_inc(m["ln"], 1)
                act.wait_ge(m["ln"], 1)
                nc.scalar.activation(y0[:, :], lnv[:, :], ACT.Exp, scale=-0.5).then_inc(m["ln"], 1)

            @block.gpsimd
            def _(pool):
                pool.wait_ge(m["peaks"], 1)
                nc.gpsimd.partition_all_reduce(allp[:, :], peaks[:, :], P, PEAK).then_inc(m["all"], 1)
                pool.wait_ge(m["v_peak"], 1)
                nc.gpsimd.partition_all_reduce(vall[:, :], vred[:, :], P, PEAK).then_inc(m["v_all"], 1)

            @block.tensor
            def _(pe):
                pe.wait_ge(m["split_lo"], 2)
                for i in range(2 * B):
                    b, r0, rows = i // 2, (0, P)[i % 2], (P, TAIL)[i % 2]
                    for half in range(2):
                        n = 2 * i + half
                        if n >= 8:
                            pe.wait_ge(m["v_out" if half else "k_out"], (n - 8) // 2 + 1)
                        todo = [(a, w, c) for c in range(DC) for a, w in ((0, 0), (0, 1), (1, 0))]
                        for q, (a, w, c) in enumerate(todo):
                            mm = nc.tensor.matmul(pk[n % 8][0:rows, :], cx[a][:, c, b, r0:r0 + rows],
                                                  kv_w[w][:, c, half * D:(half + 1) * D],
                                                  start=(q == 0), stop=(q == len(todo) - 1))
                        mm.then_inc(m["kv_ready"], 1)


def prepare_quant(nc, keep, gate_n, up_n, down_n):
    NB = FC * D // QB
    with Scope(nc, "pq") as s:
        nat = s.sb("nat", [P, 2, FC * D], F32)
        q16 = s.sb("q16", [P, FC * D], I16)
        nhi, nlo = (s.sb(n, [P, FC * D], F16) for n in ("nhi", "nlo"))
        peak, sc, rs, su = (s.sb(n, [P, NB], F32) for n in ("peak", "sc", "rs", "su"))
        red, allm, unit = (s.sb(n, [P, 1], F32) for n in ("red", "allm", "unit_w"))
        pt = [s.ps(f"pt{i}", [P, 4 * P], F16) for i in range(4)]
        loaded = [s.sem(f"loaded{i}") for i in range(3)]
        m = s.sems("red all dve scaled hi lo turned out")
        mats = [(gate_n, keep["gate"], 4), (up_n, keep["up"], 5), (down_n, keep["down"], 6)]

        with nc.Block() as block:
            @block.sync
            def _(sp):
                for i, (src, _, _) in enumerate(mats):
                    need(sp, m["lo"], i - 1)
                    sp.dma_start(nat[:, i % 2, :], src).then_inc(loaded[i], 16)

            @block.vector
            def _(dve):
                link = chain(dve, m["dve"])
                for i, (_, _, a) in enumerate(mats):
                    w = nat[:, i % 2, :].rearrange("p (n k) -> p n k", k=QB)
                    q = q16[:, :].rearrange("p (n k) -> p n k", k=QB)

                    def wide(t):
                        return t[:, :].unsqueeze(2).to_broadcast([P, NB, QB])
                    dve.wait_ge(loaded[i], 16)
                    link(nc.vector.tensor_reduce(peak[:, :], w, AX.X, ALU.max, apply_absolute_value=True))
                    link(nc.vector.tensor_scalar(sc[:, :], peak[:, :], 1.0 / WMAX, TINY, ALU.mult, ALU.max))
                    link(nc.vector.reciprocal(rs[:, :], sc[:, :]))
                    link(nc.vector.tensor_tensor(q, w, wide(rs), ALU.mult))
                    nc.vector.tensor_reduce(red[:, :], sc[:, :], AX.X, ALU.max).then_inc(m["red"], 1)
                    dve.wait_ge(m["all"], i + 1)
                    link(nc.vector.tensor_scalar(keep["alpha"][:, a:a + 1], allm[:, :], WMAX / SPAN, None, ALU.mult))
                    link(nc.vector.reciprocal(unit[:, :], keep["alpha"][:, a:a + 1]))
                    link(nc.vector.tensor_scalar(su[:, :], sc[:, :], unit[:, 0:1], None, ALU.mult))
                    nc.vector.tensor_tensor(w, q, wide(su), ALU.mult).then_inc(m["scaled"], 1)
                    dve.wait_ge(m["hi"], i + 1)
                    need(dve, m["turned"], 12 * i * 2)
                    nc.vector.tensor_tensor(nlo[:, :], nat[:, i % 2, :], nhi[:, :], ALU.subtract).then_inc(m["lo"], 1)

            @block.scalar
            def _(act):
                for i, (_, dst, _) in enumerate(mats):
                    act.wait_ge(m["scaled"], i + 1)
                    need(act, m["turned"], 12 * i * 2)
                    nc.scalar.activation(nhi[:, :], nat[:, i % 2, :], ACT.Copy).then_inc(m["hi"], 1)
                    for g in range(24):
                        part, r = g // 12, g % 12
                        act.wait_ge(m["turned"], 24 * i + g + 1)
                        out = dst[part][:, :, r * P:(r + 1) * P] if i < 2 else dst[part][:, r, :]
                        src = pt[g % 4][:, :].rearrange("p (c n) -> p c n", c=4) if i < 2 else pt[g % 4][:, :]
                        nc.scalar.activation(out, src, ACT.Copy).then_inc(m["out"], 1)

            @block.gpsimd
            def _(pool):
                for i in range(3):
                    pool.wait_ge(m["red"], i + 1)
                    nc.gpsimd.partition_all_reduce(allm[:, :], red[:, :], P, PEAK).then_inc(m["all"], 1)

            @block.tensor
            def _(pe):
                for i in range(3):
                    for g in range(24):
                        part, r = g // 12, g % 12
                        if r == 0:
                            pe.wait_ge(m["lo" if part else "hi"], i + 1)
                        need(pe, m["out"], 24 * i + g - 3)
                        src = (nlo if part else nhi)[:, :]
                        for c in range(4):
                            at = r * D + c * P if i < 2 else c * F + r * P
                            mm = nc.tensor.transpose(pt[g % 4][:, c * P:(c + 1) * P], src[:, at:at + P], keep["ident16"][:, :])
                        mm.then_inc(m["turned"], 1)


def attention(nc, keep, x, table, x1_d, hT_d, B):
    T = x.shape[0]
    NT = T // P
    U = 8
    with Scope(nc, "at") as s:
        xs = s.sb("xs", [P, U, D], F32)
        kv = s.sb("kv_rows", [P, 2, W, 2 * D], F32)
        xn, att, hn = (s.sb(n, [P, 2, D], F32) for n in ("xn", "att", "hn"))
        xhi, xlo, ahi, alo = (s.sb(n, [P, 2, DC, P], F16) for n in ("xhi", "xlo", "ahi", "alo"))
        prod, pv = s.sb("prod", [P, W, D], F32), s.sb("pv", [P, W, D], F32)
        half = s.sb("half", [P, 2, D], F32)
        hT = s.sb("hT", [P, 2, DC, BLK], F32)
        raw, sc, ds, ex, pr = (s.sb(n, [P, W, H], F32) for n in ("raw", "sc", "ds", "ex", "pr"))
        top, tot, inv = (s.sb(n, [P, H], F32) for n in ("top", "tot", "inv"))
        stats, mv = s.sb("stats2", [P, 6], F32), s.sb("mv2", [P, 2, 2], F32)
        small = s.sb("small", [P, 8], F32)
        consts = s.sb("consts", [P, 2], F32)
        psX, psA = s.ps("psX", [P, DC, P]), s.ps("psA", [P, DC, P])
        psQ = [s.ps(f"psQ{i}", [P, D]) for i in range(2)]
        psO = [s.ps(f"psO{i}", [P, D]) for i in range(2)]
        psH = [s.ps(f"psH{i}", [P, DC, P]) for i in range(2)]
        x_in, x1_out, hT_out = Transfers(s, "x_in", U), Transfers(s, "x1_out", U), Transfers(s, "hT_out", 2)
        rows_in = Transfers(s, "rows_in", 2, 16 * W)
        m = s.sems("xn xT xhi xlo q prod raw sc top ds ex tot inv pr pv half att aT ahi alo o x1 "
                         "stats mv ln0 ln1 ln2 ln3 ln4 ln5 ln6 ln6b ln7 hn hT hT_sb peak consts")
        wq, wo, ident = keep["wq"], keep["wo"], keep["ident32"]
        x_v = x.rearrange("(n p) d -> p n d", p=P)

        with nc.Block() as block:
            @block.sync
            def _(sp):
                def tick(c):
                    at, live, u = c.at, c.live, c.u
                    if live(4):
                        if u == 0:
                            x1_out.done(sp, c, -4)
                            need(sp, m["hn"], at(-3))
                        else:
                            need(sp, m["hn"], at(-3))
                            x1_out.done(sp, c, -4)
                        sp.dma_start(xs[:, (u + 4) % U, :], x_v[:, bass.ds(at(4), 1), :]).then_inc(x_in.of(c, 4), 16)
                    if live(-1):
                        need(sp, m["x1"], at(0))
                        sp.dma_start(x1_d[bass.ds(at(-1), 1), :, :].rearrange("a p d -> p (a d)"), xs[:, (u - 1) % U, :]).then_inc(x1_out.of(c, -1), 16)
                    if live(-4) and (u - 4) % 4 == 3:
                        need(sp, m["hT_sb"], at(-3))
                        sp.dma_start(hT_d[bass.ds(c.div(-4, 4), 1)].rearrange("a p d -> p (a d)"),
                                     hT[:, (u - 4) // 4 % 2].rearrange("p c t -> p (c t)")).then_inc(hT_out.sems[(u - 4) // 4 % 2], 16)
                pipeline(sp, tick, NT, U, before=4, after=4)
                x1_out.all_done(sp, NT)
                hT_out.all_done(sp, NT // 4)

            @block.scalar
            def _(act):
                act.wait_ge(m["consts"], 1)

                def tick(c):
                    at, live, u = c.at, c.live, c.u
                    if live(2):
                        x_in.done(act, c, 2)
                        need(act, m["xT"], at(1))
                        nc.scalar.activation(xn[:, u % 2, :], xs[:, (u + 2) % U, :], ACT.Identity,
                                             bias=keep["shift"][:, bass.ds(at(2), 1)],
                                             scale=keep["rstd"][:, bass.ds(at(2), 1)]).then_inc(m["xn"], 1)
                    if live(1):
                        need(act, m["xT"], at(2))
                        need(act, m["q"], at(0))
                        nc.scalar.activation(xhi[:, (u + 1) % 2], psX[:, :, :], ACT.Copy).then_inc(m["xhi"], 1)
                    if live(0):
                        need(act, m["ds"], at(1))
                        need(act, m["pr"], at(0))
                        nc.scalar.activation(ex[:, :, :], ds[:, :, :], ACT.Exp).then_inc(m["ex"], 1)
                    if live(-1):
                        need(act, m["aT"], at(0))
                        need(act, m["o"], at(-2))
                        nc.scalar.activation(ahi[:, (u - 1) % 2], psA[:, :, :], ACT.Copy).then_inc(m["ahi"], 1)
                    if live(-2):
                        need(act, m["mv"], at(-1))
                        var = mv[:, (u - 2) % 2, 1:2]
                        mean = mv[:, (u - 2) % 2, 0:1]
                        v, ln, y, yy, t, r, b = (small[:, i:i + 1] for i in range(7))
                        need(act, m["hn"], at(-2))
                        nc.scalar.activation(v, var, ACT.Identity, bias=consts[:, 0:1]).then_inc(m["ln0"], 1)
                        nc.scalar.activation(ln, var, ACT.Ln, bias=consts[:, 0:1]).then_inc(m["ln1"], 1)
                        need(act, m["ln1"], at(-1))
                        nc.scalar.activation(y, ln, ACT.Exp, scale=-0.5).then_inc(m["ln2"], 1)
                        need(act, m["ln2"], at(-1))
                        nc.scalar.activation(yy, y, ACT.Identity, scale=y).then_inc(m["ln3"], 1)
                        need(act, m["ln0"], at(-1))
                        need(act, m["ln3"], at(-1))
                        nc.scalar.activation(t, yy, ACT.Identity, scale=v).then_inc(m["ln4"], 1)
                        need(act, m["ln4"], at(-1))
                        nc.scalar.activation(b, t, ACT.Identity, scale=-0.5, bias=consts[:, 1:2]).then_inc(m["ln5"], 1)
                        need(act, m["ln5"], at(-1))
                        nc.scalar.activation(r, b, ACT.Identity, scale=y).then_inc(m["ln6"], 1)
                        need(act, m["ln6"], at(-1))
                        nc.scalar.activation(small[:, 7:8], mean, ACT.Identity, scale=r).then_inc(m["ln6b"], 1)
                        need(act, m["ln6b"], at(-1))
                        nc.scalar.activation(t, small[:, 7:8], ACT.Copy, scale=-1.0).then_inc(m["ln7"], 1)
                        need(act, m["ln7"], at(-1))
                        need(act, m["hT"], at(-3))
                        nc.scalar.activation(hn[:, (u - 2) % 2, :], xs[:, (u - 2) % U, :], ACT.Identity,
                                             bias=t, scale=r).then_inc(m["hn"], 1)
                    if live(-3):
                        need(act, m["hT"], at(-2))
                        if (u - 3) % 4 == 0:
                            need(act, hT_out.sems[(u - 3) // 4 % 2], 16 * c.div(-3, U))
                            need(act, m["peak"], at(-10))
                        nc.scalar.activation(hT[:, (u - 3) // 4 % 2, :, (u - 3) % 4 * P:((u - 3) % 4 + 1) * P],
                                             psH[(u - 3) % 2][:, :, :], ACT.Copy).then_inc(m["hT_sb"], 1)
                pipeline(act, tick, NT, U, before=2, after=3)

            @block.vector
            def _(dve):
                nc.vector.memset(consts[:, 1:2], 1.5)
                nc.vector.memset(consts[:, 0:1], EPS).then_inc(m["consts"], 1)

                def tick(c):
                    at, live, u = c.at, c.live, c.u
                    if live(1):
                        need(dve, m["xhi"], at(2))
                        nc.vector.tensor_tensor(xlo[:, (u + 1) % 2], psX[:, :, :], xhi[:, (u + 1) % 2],
                                                ALU.subtract).then_inc(m["xlo"], 1)
                    if live(0):
                        keys = kv[:, u % 2, :, 0:D]
                        rows_in.done(dve, c)
                        need(dve, m["q"], at(1))
                        nc.vector.tensor_tensor(prod[:, :, :], keys, psQ[u % 2][:, :].unsqueeze(1).to_broadcast([P, W, D]),
                                                ALU.mult).then_inc(m["prod"], 1)
                        need(dve, m["prod"], at(1))
                        nc.vector.tensor_reduce(raw[:, :, :].rearrange("p w h -> p (w h)"),
                                                prod[:, :, :].rearrange("p w (h e) -> p (w h) e", h=H),
                                                AX.X, ALU.add).then_inc(m["raw"], 1)
                        need(dve, m["raw"], at(1))
                        nc.vector.scalar_tensor_tensor(
                            out=sc[:, :, :], in0=raw[:, :, :], scalar=keep["alpha"][:, 9:10],
                            in1=keep["mask"][:, bass.ds(at(0), 1), :].rearrange("p a w -> p (a w)").unsqueeze(2).to_broadcast([P, W, H]),
                            op0=ALU.mult, op1=ALU.add).then_inc(m["sc"], 1)
                        need(dve, m["sc"], at(1))
                        nc.vector.tensor_reduce(top[:, :], sc[:, :, :].rearrange("p w h -> p h w"), AX.X,
                                                ALU.max).then_inc(m["top"], 1)
                        need(dve, m["top"], at(1))
                        nc.vector.tensor_tensor(ds[:, :, :], sc[:, :, :], top[:, :].unsqueeze(1).to_broadcast([P, W, H]),
                                                ALU.subtract).then_inc(m["ds"], 1)
                    if live(-1):
                        need(dve, m["ahi"], at(0))
                        nc.vector.tensor_tensor(alo[:, (u - 1) % 2], psA[:, :, :], ahi[:, (u - 1) % 2],
                                                ALU.subtract).then_inc(m["alo"], 1)
                    if live(0):
                        need(dve, m["ex"], at(1))
                        nc.vector.tensor_reduce(tot[:, :], ex[:, :, :].rearrange("p w h -> p h w"), AX.X,
                                                ALU.add).then_inc(m["tot"], 1)
                        need(dve, m["tot"], at(1))
                        nc.vector.reciprocal(inv[:, :], tot[:, :]).then_inc(m["inv"], 1)
                        need(dve, m["inv"], at(1))
                        nc.vector.tensor_tensor(pr[:, :, :], ex[:, :, :], inv[:, :].unsqueeze(1).to_broadcast([P, W, H]),
                                                ALU.mult).then_inc(m["pr"], 1)
                        need(dve, m["pr"], at(1))
                        need(dve, m["half"], at(0))
                        nc.vector.tensor_tensor(
                            pv[:, :, :].rearrange("p w (h e) -> p w h e", h=H),
                            kv[:, u % 2, :, D:2 * D].rearrange("p w (h e) -> p w h e", h=H),
                            pr[:, :, :].unsqueeze(3).to_broadcast([P, W, H, HD]), ALU.mult).then_inc(m["pv"], 1)
                    if live(-1):
                        need(dve, m["o"], at(0))
                        nc.vector.scalar_tensor_tensor(out=xs[:, (u - 1) % U, :], in0=psO[(u - 1) % 2][:, :],
                                                       scalar=keep["alpha"][:, 10:11], in1=xs[:, (u - 1) % U, :],
                                                       op0=ALU.mult, op1=ALU.add).then_inc(m["x1"], 1)
                        need(dve, m["x1"], at(0))
                        nc.vector.bn_stats(stats[:, :], xs[:, (u - 1) % U, :]).then_inc(m["stats"], 1)
                        need(dve, m["stats"], at(0))
                        need(dve, m["hn"], at(-2))
                    if live(-4):
                        need(dve, m["hT_sb"], at(-3))
                        nc.vector.tensor_reduce(keep["h_peak"][:, bass.ds(at(-4), 1)],
                                                hT[:, (u - 4) // 4 % 2, :, (u - 4) % 4 * P:((u - 4) % 4 + 1) * P],
                                                AX.XY, ALU.max, apply_absolute_value=True).then_inc(m["peak"], 1)
                    if live(-1):
                        nc.vector.bn_aggr(mv[:, (u - 1) % 2, :], stats[:, :]).then_inc(m["mv"], 1)
                pipeline(dve, tick, NT, U, before=1, after=4)

            @block.gpsimd
            def _(pool):
                for t in range(-1, NT):
                    if t + 1 < NT:
                        need(pool, m["pv"], t)
                        for j in range(W):
                            pool.indirect_dma_start(out=kv[:, (t + 1) % 2, j, :], out_offset=None, in_=table,
                                                    in_offset=bass.IndirectOffsetOnAxis(ap=keep["rows"][:, t + 1:t + 2], axis=0),
                                                    element_offset=j * 2 * D).then_inc(rows_in.sems[(t + 1) % 2], 16)
                    if t >= 0:
                        pool.wait_ge(m["pv"], t + 1)
                        nc.gpsimd.tensor_tensor(half[:, :, :], pv[:, 0:2, :], pv[:, 2:4, :], ALU.add).then_inc(m["half"], 1)
                        pool.wait_ge(m["half"], t + 1)
                        need(pool, m["aT"], t - 1)
                        nc.gpsimd.tensor_tensor(att[:, t % 2, :], half[:, 0, :], half[:, 1, :], ALU.add).then_inc(m["att"], 1)

            @block.tensor
            def _(pe):
                def project(out, hi, lo, w, slot):
                    todo = [(a, b, c) for c in range(DC) for a, b in ((hi, 0), (hi, 1), (lo, 0))]
                    for q, (a, b, c) in enumerate(todo):
                        mm = nc.tensor.matmul(out[:, :], a[:, slot, c, :], w[b][:, c, :],
                                              start=(q == 0), stop=(q == len(todo) - 1))
                    return mm

                def tick(c):
                    at, live, u = c.at, c.live, c.u
                    if live(1):
                        need(pe, m["xn"], at(2))
                        need(pe, m["xlo"], at(1))
                        for c in range(DC):
                            mm = nc.tensor.transpose(psX[:, c, :], xn[:, (u + 1) % 2, c * P:(c + 1) * P], ident[:, :])
                        mm.then_inc(m["xT"], 1)
                        need(pe, m["xlo"], at(2))
                        need(pe, m["prod"], at(0))
                        project(psQ[(u + 1) % 2], xhi, xlo, wq, (u + 1) % 2).then_inc(m["q"], 1)
                    if live(-1):
                        need(pe, m["att"], at(0))
                        need(pe, m["alo"], at(-1))
                        for c in range(DC):
                            mm = nc.tensor.transpose(psA[:, c, :], att[:, (u - 1) % 2, c * P:(c + 1) * P], ident[:, :])
                        mm.then_inc(m["aT"], 1)
                        need(pe, m["alo"], at(0))
                        need(pe, m["x1"], at(-2))
                        project(psO[(u - 1) % 2], ahi, alo, wo, (u - 1) % 2).then_inc(m["o"], 1)
                    if live(-2):
                        need(pe, m["hn"], at(-1))
                        need(pe, m["hT_sb"], at(-3))
                        for c in range(DC):
                            mm = nc.tensor.transpose(psH[u % 2][:, c, :], hn[:, u % 2, c * P:(c + 1) * P], ident[:, :])
                        mm.then_inc(m["hT"], 1)
                pipeline(pe, tick, NT, U, before=1, after=2)


def whole_peak(nc, s, m, name, cols):
    red, out = s.sb(f"{name}_red", [P, 1], F32), s.sb(f"{name}_all", [P, 1], F32)

    def on_vector(dve):
        nc.vector.tensor_reduce(red[:, :], cols, AX.X, ALU.max).then_inc(m[f"{name}_red"], 1)

    def on_pool(pool):
        pool.wait_ge(m[f"{name}_red"], 1)
        nc.gpsimd.partition_all_reduce(out[:, :], red[:, :], P, PEAK).then_inc(m[f"{name}_all"], 1)
    return out, on_vector, on_pool


def quantiser(nc, link, scale, inv, peak, unit):
    link(nc.vector.tensor_scalar(scale, peak, unit, 1.0 / QMAX, ALU.mult, ALU.mult))
    link(nc.vector.tensor_scalar(scale, scale, TINY, None, ALU.max))
    link(nc.vector.reciprocal(inv, scale))
    link(nc.vector.tensor_tensor(inv, inv, unit, ALU.mult))


def feed_in(nc, keep, hT_d, raw_d, NB, gate_d=None):
    up = gate_d is not None
    name = "up" if up else "ga"
    wt = keep["up" if up else "gate"]
    g = keep["g"]
    U = 2
    PAIRS = FC // 2
    with Scope(nc, name) as s:
        hb = s.sb("hb", [P, 2, DC * BLK], F32)
        hq = s.sb("hq", [P, DC * BLK], I16)
        ah, al = (s.sb(n, [P, 2, DC, BLK], F16) for n in ("ah", "al"))
        raw = s.sb("raw", [P, 3, UE], F32)
        pp = [s.ps(f"pp{i}", [P, 2, BLK]) for i in range(4)]
        h_in, stored = Transfers(s, "h_in", 2), Transfers(s, "stored", UNITS)
        gate_in, gate_out = Transfers(s, "gate_in", 3), Transfers(s, "gate_out", 2)
        m = s.sems("h_red h_all g_red g_all dve scales hq ah al mm out peak gq sig sq prod gpeak")
        if up:
            gin, gp = s.sb("gin", [P, 3, UE], F32), s.sb("gp", [P, 2, UE], F32)
            sig = s.sb("sig", [P, 2, UE], F32)
            gq, sq = s.sb("gq", [P, 2, UE], I16), s.sb("sq", [P, 2, UE], U16)
            gate_u = gate_d.rearrange("b q p d -> (b q) p d")
            peak, peak_v, peak_p = whole_peak(nc, s, m, "g", keep["gate_peak"][:, :])
        else:
            peak, peak_v, peak_p = whole_peak(nc, s, m, "h", keep["h_peak"][:, :])
            gate_u = None
        out_peak = keep["up_peak" if up else "gate_peak"]

        with nc.Block() as block:
            @block.sync
            def _(sp):
                def tick(c):
                    at, live, u = c.at, c.live, c.u
                    if live(1):
                        need(sp, m["hq"], at(0))
                        sp.dma_start(hb[:, (u + 1) % 2, :], hT_d[bass.ds(at(1), 1)].rearrange("a p d -> p (a d)")).then_inc(h_in.of(c, 1), 16)
                    for q in range(UNITS):
                        n = at(0) * UNITS + q
                        if up and c.live_unit(UNITS, q + 3):
                            need(sp, m["gq"], n + 1)
                            sp.dma_start(gin[:, q, :], gate_u[bass.ds(n + 3, 1)].rearrange("a p d -> p (a d)")).then_inc(gate_in.of(c, 0, UNITS, q + 3), 16)
                        if up and c.live_unit(UNITS, q + 1):
                            need(sp, m["gpeak"], n + 2)
                            sp.dma_start(gate_u[bass.ds(n + 1, 1)].rearrange("a p d -> p (a d)"),
                                         gp[:, (u * UNITS + q + 1) % 2, :]).then_inc(gate_out.of(c, 0, UNITS, q + 1), 16)
                        if live(0):
                            need(sp, m["peak"], n + 1)
                            sp.dma_start(raw_d[bass.ds(at(0), 1), q].rearrange("a p d -> p (a d)"), raw[:, q, :]).then_inc(stored.of(c, 0, UNITS, q), 16)
                pipeline(sp, tick, NB, U, before=1)
                stored.all_done(sp, UNITS * NB)
                if up:
                    gate_out.all_done(sp, UNITS * NB)

            @block.gpsimd
            def _(pool):
                peak_p(pool)

            @block.vector
            def _(dve):
                link = chain(dve, m["dve"])
                peak_v(dve)
                if not up:
                    dve.wait_ge(m["h_all"], 1)
                    link(nc.vector.memset(g[:, 15:16], 1.0))
                    quantiser(nc, link, g[:, 0:1], g[:, 1:2], peak[:, :], g[:, 15:16])
                    link(nc.vector.tensor_tensor(g[:, 2:3], g[:, 0:1], keep["alpha"][:, 4:5], ALU.mult))
                    link(nc.vector.tensor_tensor(g[:, 3:4], g[:, 0:1], keep["alpha"][:, 5:6], ALU.mult))
                else:
                    dve.wait_ge(m["g_all"], 1)
                    quantiser(nc, link, g[:, 4:5], g[:, 5:6], peak[:, :], g[:, 2:3])
                nc.vector.memset(g[:, 14:15], 0.0).then_inc(m["scales"], 1)

                def tick(c):
                    at, live, u = c.at, c.live, c.u
                    if live(1):
                        a = (u + 1) % 2
                        need(dve, m["hq"], at(2))
                        need(dve, m["mm"], at(0) * PAIRS)
                        nc.vector.tensor_copy(ah[:, a].rearrange("p c t -> p (c t)"), hq[:, :]).then_inc(m["ah"], 1)
                        need(dve, m["ah"], at(2))
                        nc.vector.tensor_tensor(al[:, a].rearrange("p c t -> p (c t)"), hq[:, :],
                                                ah[:, a].rearrange("p c t -> p (c t)"), ALU.subtract).then_inc(m["al"], 1)
                    for q in range(UNITS):
                        n = at(0) * UNITS + q
                        if up and c.live_unit(UNITS, q + 1):
                            k = (u * UNITS + q + 1) % 2
                            need(dve, m["sig"], n + 2)
                            need(dve, m["prod"], n)
                            nc.vector.tensor_scalar(sq[:, k, :], sig[:, k, :], 65536.0, 65535.0, ALU.mult, ALU.min).then_inc(m["sq"], 1)
                            need(dve, m["sq"], n + 2)
                            gate_out.done(dve, c, 0, UNITS, q - 1)
                            nc.vector.tensor_tensor(gp[:, k, :], gq[:, k, :], sq[:, k, :], ALU.mult).then_inc(m["prod"], 1)
                            need(dve, m["prod"], n + 2)
                            nc.vector.tensor_reduce(keep["gated_peak"][:, bass.ds(n + 1, 1)], gp[:, k, :], AX.X, ALU.max,
                                                    apply_absolute_value=True).then_inc(m["gpeak"], 1)
                        if live(0):
                            need(dve, m["out"], n * 2 + 2)
                            nc.vector.tensor_reduce(out_peak[:, bass.ds(n, 1)], raw[:, q, :], AX.X, ALU.max,
                                                    apply_absolute_value=True).then_inc(m["peak"], 1)
                pipeline(dve, tick, NB, U, before=1)

            @block.scalar
            def _(act):
                act.wait_ge(m["scales"], 1)

                def tick(c):
                    at, live, u = c.at, c.live, c.u
                    def quantise_next():
                        if live(1):
                            h_in.done(act, c, 1)
                            need(act, m["al"], at(1))
                            nc.scalar.activation(hq[:, :], hb[:, (u + 1) % 2, :], ACT.Copy, scale=g[:, 1:2]).then_inc(m["hq"], 1)
                    if not live(0):
                        quantise_next()
                    for q in range(UNITS):
                        n = at(0) * UNITS + q
                        if up and c.live_unit(UNITS, q + 1):
                            k = (u * UNITS + q + 1) % 2
                            gate_in.done(act, c, 0, UNITS, q + 1)
                            need(act, m["prod"], n)
                            nc.scalar.activation(gq[:, k, :], gin[:, (q + 1) % 3, :], ACT.Copy, scale=g[:, 5:6]).then_inc(m["gq"], 1)
                            need(act, m["gq"], n + 2)
                            need(act, m["sq"], n)
                            nc.scalar.activation(sig[:, k, :], gq[:, k, :], ACT.Sigmoid, scale=g[:, 4:5]).then_inc(m["sig"], 1)
                        if not live(0):
                            continue
                        for h in range(2):
                            pair = 2 * q + h
                            need(act, m["mm"], at(0) * PAIRS + pair + 1)
                            if h == 0:
                                stored.done(act, c, 0, UNITS, q - UNITS)
                            nc.scalar.activation(raw[:, q, h * 2 * BLK:(h + 1) * 2 * BLK],
                                                 pp[(u * PAIRS + pair) % 4][:, :, :].rearrange("p a t -> p (a t)"),
                                                 ACT.Copy).then_inc(m["out"], 1)
                        if q == 0:
                            quantise_next()
                pipeline(act, tick, NB, U, before=1)

            @block.tensor
            def _(pe):
                def tick(c):
                    at, live, u = c.at, c.live, c.u
                    need(pe, m["al"], at(1))
                    for pair in range(PAIRS):
                        need(pe, m["out"], at(0) * PAIRS + pair - 3)
                        bank = pp[(u * PAIRS + pair) % 4]
                        for h in range(2):
                            f = (2 * pair + h) * P
                            todo = [(w, a, c) for c in range(DC) for w, a in ((0, ah), (0, al), (1, ah))]
                            for q, (w, a, c) in enumerate(todo):
                                mm = nc.tensor.matmul(bank[:, h, :], wt[w][:, c, f:f + P], a[:, u % 2, c, :],
                                                      start=(q == 0), stop=(q == len(todo) - 1))
                        mm.then_inc(m["mm"], 1)
                pipeline(pe, tick, NB, U)


def product_peak(nc, keep, gate_d, up_d, NB):
    g = keep["g"]
    N, U = NB * UNITS, 4
    gv, uv = (t.rearrange("b q p d -> (b q) p d") for t in (gate_d, up_d))
    with Scope(nc, "pp") as s:
        gi, ui = s.sb("gi", [P, 4, UE], F32), s.sb("ui", [P, 4, UE], F32)
        ga, ua = s.sb("ga", [P, 2, UE], I16), s.sb("ua", [P, 2, UE], I16)
        junk = s.sb("junk", [P, UE], F32)
        col = s.sb("col", [P, 4], F32)
        gin, uin = Transfers(s, "gin", 4), Transfers(s, "uin", 4)
        m = s.sems("g_red g_all u_red u_all dve scales ga ua prod col")
        pg, pg_v, pg_p = whole_peak(nc, s, m, "g", keep["gated_peak"][:, :])
        pu, pu_v, pu_p = whole_peak(nc, s, m, "u", keep["up_peak"][:, :])

        with nc.Block() as block:
            @block.sync
            def _(sp):
                def tick(c):
                    at, live, u = c.at, c.live, c.u
                    if live(3):
                        need(sp, m["ga"], at(0))
                        sp.dma_start(gi[:, (u + 3) % 4, :], gv[bass.ds(at(3), 1)].rearrange("a p d -> p (a d)")).then_inc(gin.of(c, 3), 16)
                        need(sp, m["ua"], at(0))
                        sp.dma_start(ui[:, (u + 3) % 4, :], uv[bass.ds(at(3), 1)].rearrange("a p d -> p (a d)")).then_inc(uin.of(c, 3), 16)
                pipeline(sp, tick, N, U, before=3)

            @block.gpsimd
            def _(pool):
                pg_p(pool)
                pu_p(pool)

            @block.scalar
            def _(act):
                act.wait_ge(m["scales"], 1)

                def tick(c):
                    at, live, u = c.at, c.live, c.u
                    gin.done(act, c)
                    need(act, m["prod"], at(-1))
                    nc.scalar.activation(ga[:, u % 2, :], gi[:, u % 4, :], ACT.Abs, scale=g[:, 7:8]).then_inc(m["ga"], 1)
                    uin.done(act, c)
                    nc.scalar.activation(ua[:, u % 2, :], ui[:, u % 4, :], ACT.Abs, scale=g[:, 10:11]).then_inc(m["ua"], 1)
                pipeline(act, tick, N, U)

            @block.vector
            def _(dve):
                link = chain(dve, m["dve"])
                pg_v(dve)
                pu_v(dve)
                link(nc.vector.tensor_scalar(g[:, 6:7], g[:, 4:5], 1.0 / 65536.0, None, ALU.mult))
                dve.wait_ge(m["g_all"], 1)
                quantiser(nc, link, g[:, 8:9], g[:, 7:8], pg[:, :], g[:, 6:7])
                dve.wait_ge(m["u_all"], 1)
                quantiser(nc, link, g[:, 9:10], g[:, 10:11], pu[:, :], g[:, 3:4])
                nc.vector.tensor_tensor(g[:, 11:12], g[:, 8:9], g[:, 9:10], ALU.mult).then_inc(m["scales"], 1)

                def tick(c):
                    at, live, u = c.at, c.live, c.u
                    if live(0):
                        need(dve, m["ua"], at(1))
                        need(dve, m["ga"], at(1))
                        need(dve, m["col"], at(-1))
                    if live(-1):
                        need(dve, m["prod"], at(0))
                        nc.vector.tensor_copy(keep["o_peak"][:, bass.ds(at(-1), 1)], col[:, (u - 1) % 4:(u - 1) % 4 + 1]).then_inc(m["col"], 1)
                    if live(0):
                        nc.vector.tensor_tensor_reduce(out=junk[:, :], in0=ga[:, u % 2, :], in1=ua[:, u % 2, :], scale=1.0,
                                                       scalar=0.0, op0=ALU.mult, op1=ALU.max,
                                                       accum_out=col[:, u % 4:u % 4 + 1]).then_inc(m["prod"], 1)
                pipeline(dve, tick, N, U, after=1)


def feed_out(nc, keep, gate_d, up_d, x1_d, out, NB):
    g = keep["g"]
    wt = keep["down"]
    U = 2
    out_v = out.rearrange("(b n p) d -> b p n d", p=P, n=SUB)
    x1_v = x1_d.rearrange("(b n) p d -> b p n d", n=SUB)
    gate_u, up_u = (d.rearrange("b q p d -> (b q) p d") for d in (gate_d, up_d))
    with Scope(nc, "fo") as s:
        gi, ui = s.sb("gi", [P, 3, UE], F32), s.sb("ui", [P, 3, UE], F32)
        gq, uq = (s.sb(n, [P, 2, UE], I16) for n in ("gq", "uq"))
        oq = s.sb("oq", [P, UE], I16)
        o = s.sb("o", [P, UE], F32)
        oh, ol = (s.sb(n, [P, 2, FC, BLK], F16) for n in ("oh", "ol"))
        xb = s.sb("xb", [P, 2, SUB, D], F32)
        py = [s.ps(f"py{i}", [P, D]) for i in range(8)]
        gin, uin = Transfers(s, "gin", 3), Transfers(s, "uin", 3)
        x_in, stored = Transfers(s, "x_in", 2), Transfers(s, "stored", 2)
        m = s.sems("o_red o_all dve scales gq uq o oq oh ol mm y")
        po, po_v, po_p = whole_peak(nc, s, m, "o", keep["o_peak"][:, :])

        with nc.Block() as block:
            @block.sync
            def _(sp):
                def tick(c):
                    at, live, u = c.at, c.live, c.u
                    if live(-1):
                        need(sp, m["y"], at(0) * SUB)
                        sp.dma_start(out_v[bass.ds(at(-1), 1)].rearrange("a p n d -> p (a n) d"), xb[:, (u + 1) % 2]).then_inc(stored.of(c, -1), 16)
                    if live(1):
                        stored.done(sp, c, -1)
                        sp.dma_start(xb[:, (u + 1) % 2], x1_v[bass.ds(at(1), 1)].rearrange("a p n d -> p (a n) d")).then_inc(x_in.of(c, 1), 16)
                    for q in range(UNITS):
                        n = at(0) * UNITS + q
                        if c.live_unit(UNITS, q + 4):
                            k = (q + 4) % 3
                            need(sp, m["gq"], n + 2)
                            sp.dma_start(gi[:, k, :], gate_u[bass.ds(n + 4, 1)].rearrange("a p d -> p (a d)")).then_inc(gin.of(c, 0, UNITS, q + 4), 16)
                            need(sp, m["uq"], n + 2)
                            sp.dma_start(ui[:, k, :], up_u[bass.ds(n + 4, 1)].rearrange("a p d -> p (a d)")).then_inc(uin.of(c, 0, UNITS, q + 4), 16)
                pipeline(sp, tick, NB, U, before=2, after=1)
                stored.all_done(sp, NB)

            @block.gpsimd
            def _(pool):
                po_p(pool)

            @block.scalar
            def _(act):
                act.wait_ge(m["scales"], 1)

                def tick(c):
                    at, live, u = c.at, c.live, c.u
                    for q in range(UNITS):
                        n = at(0) * UNITS + q
                        if c.live_unit(UNITS, q + 4):
                            k = (u * UNITS + q) % 2
                            gin.done(act, c, 0, UNITS, q + 4)
                            need(act, m["o"], n + 3)
                            nc.scalar.activation(gq[:, k, :], gi[:, (q + 4) % 3, :], ACT.Copy, scale=g[:, 7:8]).then_inc(m["gq"], 1)
                            uin.done(act, c, 0, UNITS, q + 4)
                            nc.scalar.activation(uq[:, k, :], ui[:, (q + 4) % 3, :], ACT.Copy, scale=g[:, 10:11]).then_inc(m["uq"], 1)
                        if c.live_unit(UNITS, q + 3):
                            need(act, m["o"], n + 4)
                            need(act, m["ol"], n + 3)
                            nc.scalar.activation(oq[:, :], o[:, :], ACT.Copy, scale=g[:, 13:14]).then_inc(m["oq"], 1)
                pipeline(act, tick, NB, U, before=2)

            @block.vector
            def _(dve):
                link = chain(dve, m["dve"])
                po_v(dve)
                dve.wait_ge(m["o_all"], 1)
                quantiser(nc, link, g[:, 12:13], g[:, 13:14], po[:, :], g[:, 11:12])
                nc.vector.tensor_tensor(g[:, 14:15], g[:, 12:13], keep["alpha"][:, 6:7], ALU.mult).then_inc(m["scales"], 1)
                dve.wait_ge(m["scales"], 1)

                def tick(c):
                    at, live, u = c.at, c.live, c.u

                    def sum_out(t):
                        n = at(0) * SUB + t
                        need(dve, m["mm"], n + 1)
                        if t == 0:
                            x_in.done(dve, c)
                        nc.vector.scalar_tensor_tensor(out=xb[:, u % 2, t, :], in0=py[(u * SUB + t) % 8][:, :],
                                                       scalar=g[:, 14:15], in1=xb[:, u % 2, t, :],
                                                       op0=ALU.mult, op1=ALU.add).then_inc(m["y"], 1)
                    for q in range(UNITS):
                        n = at(0) * UNITS + q
                        if c.live_unit(UNITS, q + 3):
                            f = (q + 3) % UNITS
                            b = (u + (q + 3) // UNITS) % 2
                            hi = oh[:, b, f * UN:(f + 1) * UN, :].rearrange("p f t -> p (f t)")
                            lo = ol[:, b, f * UN:(f + 1) * UN, :].rearrange("p f t -> p (f t)")
                            need(dve, m["oq"], n + 4)
                            if q == 0:
                                need(dve, m["mm"], at(0) * SUB)
                            nc.vector.tensor_copy(hi, oq[:, :]).then_inc(m["oh"], 1)
                        if c.live_unit(UNITS, q + 4):
                            k = (u * UNITS + q) % 2
                            need(dve, m["gq"], n + 5)
                            need(dve, m["uq"], n + 5)
                            need(dve, m["oq"], n + 4)
                            nc.vector.tensor_tensor(o[:, :], gq[:, k, :], uq[:, k, :], ALU.mult).then_inc(m["o"], 1)
                        if c.live_unit(UNITS, q + 3):
                            need(dve, m["oh"], n + 4)
                            nc.vector.tensor_tensor(lo, oq[:, :], hi, ALU.subtract).then_inc(m["ol"], 1)
                        if live(0):
                            sum_out(q)
                    if live(0):
                        sum_out(SUB - 1)
                pipeline(dve, tick, NB, U, before=2)

            @block.tensor
            def _(pe):
                def tick(c):
                    at, live, u = c.at, c.live, c.u
                    need(pe, m["ol"], at(1) * UNITS)
                    for t in range(SUB):
                        need(pe, m["y"], at(0) * SUB + t - 7)
                        todo = [(a, w, f) for f in range(FC) for a, w in ((oh, 0), (oh, 1), (ol, 0))]
                        for q, (a, w, f) in enumerate(todo):
                            mm = nc.tensor.matmul(py[(u * SUB + t) % 8][:, :], a[:, u % 2, f, t * P:(t + 1) * P],
                                                  wt[w][:, f, :], start=(q == 0), stop=(q == len(todo) - 1))
                        mm.then_inc(m["mm"], 1)
                pipeline(pe, tick, NB, U)


def identity(nc, keep):
    with Scope(nc, "id") as s:
        made = s.sem("made")
        with nc.Block() as block:
            @block.gpsimd
            def _(pool):
                nc.gpsimd.memset(keep["ident32"][:, :], 0.0).then_inc(made, 1)
                pool.wait_ge(made, 1)
                nc.gpsimd.affine_select(out=keep["ident32"][:, :], in_=keep["ident32"][:, :], compare_op=ALU.not_equal,
                                        fill=1.0, base=0, pattern=[[-1, P]], channel_multiplier=1).then_inc(made, 1)
                pool.wait_ge(made, 2)
                nc.gpsimd.tensor_copy(keep["ident16"][:, :], keep["ident32"][:, :]).then_inc(made, 1)
                pool.wait_ge(made, 3)


def build(nc, x, ctx_t, idx_t, wq_t, wkv_t, wo_t, gate_n, up_n, down_n, out, B, LKV):
    T = x.shape[0]
    NT, NB = T // P, T // BLK
    table = nc.dram_tensor("kv_table", [B * (LKV + 6), 2 * D], F32).ap()
    x1_d = nc.dram_tensor("x1_scratch", [NT, P, D], F32).ap()
    hT_d = nc.dram_tensor("hT_scratch", [NB, P, DC * BLK], F32).ap()
    gate_d = nc.dram_tensor("gate_scratch", [NB, UNITS, P, UE], F32).ap()
    up_d = nc.dram_tensor("up_scratch", [NB, UNITS, P, UE], F32).ap()
    U3 = NB * UNITS
    with Scope(nc, "kept") as s:
        keep = {
            "down": [s.sb(f"down{i}", [P, FC, D], F16) for i in range(2)],
            "alpha": s.sb("alpha", [P, 12], F32),
            "g": s.sb("g", [P, 16], F32),
            "h_peak": s.sb("h_peak", [P, NT], F32), "gate_peak": s.sb("gate_peak", [P, U3], F32),
            "up_peak": s.sb("up_peak", [P, U3], F32), "gated_peak": s.sb("gated_peak", [P, U3], F32),
            "o_peak": s.sb("o_peak", [P, U3], F32),
        }
        with Scope(nc, "kept") as s_up:
            keep["up"] = [s_up.sb(f"up{i}", [P, DC, F], F16) for i in range(2)]
            with Scope(nc, "kept") as s_gate:
                keep["gate"] = [s_gate.sb(f"gate{i}", [P, DC, F], F16) for i in range(2)]
                with Scope(nc, "kept") as s_att:
                    for n in ("wq", "wo"):
                        keep[n] = [s_att.sb(f"{n}{i}", [P, DC, D], F16) for i in range(2)]
                    for n, shape, dt in (("ident32", [P, P], F32), ("ident16", [P, P], F16), ("rows", [P, NT], I32),
                                         ("mask", [P, NT, W], F32), ("rstd", [P, NT], F32), ("shift", [P, NT], F32)):
                        keep[n] = s_att.sb(n, shape, dt)
                    identity(nc, keep)
                    prepare_dense(nc, keep, x, ctx_t, idx_t, wq_t, wkv_t, wo_t, table, B, LKV)
                    prepare_quant(nc, keep, gate_n, up_n, down_n)
                    attention(nc, keep, x, table, x1_d, hT_d, B)
                feed_in(nc, keep, hT_d, gate_d, NB)
            feed_in(nc, keep, hT_d, up_d, NB, gate_d)
        product_peak(nc, keep, gate_d, up_d, NB)
        feed_out(nc, keep, gate_d, up_d, x1_d, out, NB)


def kernel(x, ctx_1024, itok_BxS_0_511, L0_xattn_Wq, L0_xattn_Wkv, L0_xattn_Wo, L0_ffn_w_gate, L0_ffn_w_up,
           L0_ffn_w_down):
    import numpy as np
    import concourse.bacc as bacc
    from concourse import mybir
    from concourse.bass_utils import run_bass_kernel_spmd

    B, LQ, _ = x.shape
    LKV = ctx_1024.shape[1]

    def contraction_first(w):
        w = np.asarray(w)
        return np.ascontiguousarray(w.T.reshape(DC, P, -1).transpose(1, 0, 2)).reshape(P, -1)

    def by_partition(w):
        w = np.asarray(w)
        return np.ascontiguousarray(w.reshape(-1, P, w.shape[1]).transpose(1, 0, 2)).reshape(P, -1)

    arrays = {
        "x": np.ascontiguousarray(np.asarray(x).reshape(B * LQ, D)),
        "ctx_t": contraction_first(np.asarray(ctx_1024).reshape(B * LKV, D)),
        "idx_t": np.ascontiguousarray(np.asarray(itok_BxS_0_511).reshape(-1, P).T),
        "wq_t": contraction_first(L0_xattn_Wq), "wkv_t": contraction_first(L0_xattn_Wkv),
        "wo_t": contraction_first(L0_xattn_Wo), "gate_n": by_partition(L0_ffn_w_gate),
        "up_n": by_partition(L0_ffn_w_up), "down_n": by_partition(L0_ffn_w_down),
    }
    nc = bacc.Bacc("TRN2", target_bir_lowering=False, num_devices=1)
    args = [nc.dram_tensor(f"in_{n}", a.shape, mybir.dt.from_np(a.dtype), kind="ExternalInput").ap()
            for n, a in arrays.items()]
    out = nc.dram_tensor("out", (B * LQ, D), mybir.dt.float32, kind="ExternalOutput").ap()
    build(nc, *args, out, B, LKV)
    r = run_bass_kernel_spmd(nc, [{f"in_{n}": a for n, a in arrays.items()}], core_ids=[0])
    return r.results[0]["out"].reshape(B, LQ, D)
```

```python
from contextlib import ExitStack

import concourse.bass as bass
from concourse import mybir

F32 = mybir.dt.float32
F16 = mybir.dt.float16
I16 = mybir.dt.int16
U16 = mybir.dt.uint16
I32 = mybir.dt.int32
ALU = mybir.AluOpType
ACT = mybir.ActivationFunctionType
AX = mybir.AxisListType
PEAK = bass.bass_isa.ReduceOp.max

P = 128
D = 512
DC = D // P
H, HD = 16, 32
W = 4
F = 1536
FC = F // P
QB = 32
BLK = 512
SUB = BLK // P
EPS = 1e-5
QMAX = 32767.0
WMAX = 7.0
TINY = 1e-12
SPAN = 1024.0
VSPAN = 64.0
LOW = -3.0e38
UN = 4
UNITS = FC // UN
UE = UN * BLK


def need(eng, sem, value):
    if isinstance(value, int) and value <= 0:
        return
    eng.wait_ge(sem, value)


class Tick:

    def __init__(self, n, unroll, u, k=None, s=None):
        self.n, self.unroll, self.u, self.k, self.s = n, unroll, u, k, s

    def at(self, off=0):
        return self.div(off, 1)

    def div(self, off, m, per=1, add=0):
        if self.k is None:
            return ((self.s + off) * per + add) // m
        assert self.unroll * per % m == 0
        return self.k * (self.unroll * per // m) + ((self.u + off) * per + add) // m

    def live(self, off=0):
        return self.k is not None or 0 <= self.s + off < self.n

    def live_unit(self, per, add):
        return self.k is not None or 0 <= self.s * per + add < self.n * per


def pipeline(eng, tick, n, unroll, before=0, after=0):
    assert n % unroll == 0 and n // unroll >= 3 and before <= unroll and after <= unroll
    for s in range(-before, unroll):
        tick(Tick(n, unroll, s % unroll, s=s))
    with eng.Fori(1, n // unroll - 1) as k:
        for u in range(unroll):
            tick(Tick(n, unroll, u, k=k))
    for s in range(n - unroll, n + after):
        tick(Tick(n, unroll, s % unroll, s=s))


class Transfers:

    def __init__(self, scope, name, slots, each=16):
        self.sems, self.slots, self.each = [scope.sem(f"{name}{i}") for i in range(slots)], slots, each

    def of(self, c, off=0, per=1, add=0):
        return self.sems[((c.u + off) * per + add) % self.slots]

    def done(self, eng, c, off=0, per=1, add=0):
        need(eng, self.of(c, off, per, add), self.each * (c.div(off, self.slots, per, add) + 1))

    def all_done(self, eng, n):
        for i, sem in enumerate(self.sems):
            need(eng, sem, self.each * ((n - i + self.slots - 1) // self.slots))


class Scope:

    def __init__(self, nc, tag):
        self.nc, self.tag, self.ctx, self.own = nc, tag, ExitStack(), []

    def __enter__(self):
        self.ctx.__enter__()
        return self

    def __exit__(self, *a):
        if self.own and a[0] is None:
            self.nc.clear_and_free_semaphores(self.own)
            self.nc.all_engine_barrier()
        return self.ctx.__exit__(*a)

    def sb(self, name, shape, dt):
        return self.ctx.enter_context(self.nc.sbuf_tensor(f"{self.tag}_{name}", shape, dt))

    def ps(self, name, shape, dt=F32):
        return self.ctx.enter_context(self.nc.psum_tensor(f"{self.tag}_{name}", shape, dt))

    def sem(self, name):
        self.own.append(self.nc.alloc_semaphore(f"{self.tag}_{name}"))
        return self.own[-1]

    def sems(self, names):
        return {n: self.sem(n) for n in names.split()}


def chain(eng, sem):
    count = [0]

    def link(ins):
        count[0] += 1
        ins.then_inc(sem, 1)
        eng.wait_ge(sem, count[0])
    return link


def prepare_dense(nc, keep, x, ctx_t, idx_t, wq_t, wkv_t, wo_t, table, B, LKV):
    T = x.shape[0]
    NT = T // P
    PER = NT // B
    ROWS = LKV + 6
    TAIL = LKV - P
    XG = 2
    with Scope(nc, "pd") as s:
        fq, fo = s.sb("fq", [P, DC * D], F32), s.sb("fo", [P, DC * D], F32)
        fkv, fc = s.sb("fkv", [P, DC * 2 * D], F32), s.sb("fc", [P, DC * B * LKV], F32)
        kv_w = [s.sb(f"kv_w{i}", [P, DC, 2 * D], F16) for i in range(2)]
        cx = [s.sb(f"cx{i}", [P, DC, B, LKV], F16) for i in range(2)]
        kv = s.sb("kv", [P, 2 * B, 2 * D], F32)
        xg = s.sb("xg", [P, 2, XG, D], F32)
        peaks, allp, unit = s.sb("peaks", [P, 4], F32), s.sb("allp", [P, 4], F32), s.sb("unit", [P, 4], F32)
        vcol, vred, vall, vinv = (s.sb(n, [P, m], F32) for n, m in (("vcol", 2 * B), ("vred", 1), ("vall", 1), ("vinv", 1)))
        stats, mv = s.sb("stats", [P, NT, 6], F32), s.sb("mv", [P, NT, 2], F32)
        veps, lnv, y0, y1, y2 = (s.sb(n, [P, NT], F32) for n in ("veps", "lnv", "y0", "y1", "y2"))
        ids, idf = s.sb("ids", [P, NT], I32), s.sb("idf", [P, NT], F32)
        pk = [s.ps(f"pk{i}", [P, D]) for i in range(8)]
        m = s.sems("ids peaks all unit split_hi split_lo kv_ready k_out v_out v_peak v_all v_scaled "
                         "stat ln dve rows_out veps")
        loads = [(fq, wq_t, keep["wq"]), (fo, wo_t, keep["wo"]), (fkv, wkv_t, None), (fc, ctx_t, None)]
        x_loaded = [s.sem(f"x_loaded{i}") for i in range(2)]
        mat_in = [s.sem(f"mat_in{i}") for i in range(4)]
        pairs = [(keep["wq"], fq), (keep["wo"], fo), (kv_w, fkv), (cx, fc)]

        def flat(t):
            return t.rearrange("p a b c -> p (a b c)") if len(t.shape) == 4 else t.rearrange("p a b -> p (a b)")

        with nc.Block() as block:
            @block.sync
            def _(sp):
                sp.dma_start(ids[:, :], idx_t).then_inc(m["ids"], 16)
                for i in (3, 2, 0, 1):
                    sp.dma_start(loads[i][0][:, :], loads[i][1]).then_inc(mat_in[i], 16)
                for g in range(NT // XG):
                    need(sp, m["stat"], (g - 1) * XG)
                    sp.dma_start(xg[:, g % 2], x[g * XG * P:(g + 1) * XG * P, :].rearrange(
                        "(n p) d -> p n d", p=P)).then_inc(x_loaded[g % 2], 16)
                sp.wait_ge(m["v_scaled"], 1)
                for b in range(B):
                    lo, hi = kv[:, 2 * b, :], kv[:, 2 * b + 1, :]
                    sp.dma_start(table[b * ROWS + 3:b * ROWS + 3 + P, :], lo).then_inc(m["rows_out"], 16)
                    sp.dma_start(table[b * ROWS + 3 + P:b * ROWS + 3 + LKV, :], hi[0:TAIL]).then_inc(m["rows_out"], 16)
                    for j in range(3):
                        sp.dma_start(table[b * ROWS + j:b * ROWS + j + 1, :], lo[0:1]).then_inc(m["rows_out"], 16)
                        sp.dma_start(table[b * ROWS + 3 + LKV + j:b * ROWS + 4 + LKV + j, :],
                                     hi[TAIL - 1:TAIL]).then_inc(m["rows_out"], 16)
                sp.wait_ge(m["rows_out"], 16 * 8 * B)

            @block.vector
            def _(dve):
                link = chain(dve, m["dve"])
                for i, (f, _, _) in enumerate(loads):
                    dve.wait_ge(mat_in[i], 16)
                    last = nc.vector.tensor_reduce(peaks[:, i:i + 1], f[:, :], AX.X, ALU.max, apply_absolute_value=True)
                last.then_inc(m["peaks"], 1)
                link(nc.vector.memset(vcol[:, :], 0.0))
                dve.wait_ge(m["ids"], 16)
                link(nc.vector.tensor_scalar(idf[:, :], ids[:, :], 0.0, float(LKV + 2), ALU.max, ALU.min))
                for j in range(W):
                    nc.vector.tensor_scalar(keep["mask"][:, :, j], idf[:, :], float(3 - j), LOW, ALU.is_lt, ALU.mult)
                for b in range(B):
                    link(nc.vector.tensor_scalar(keep["rows"][:, b * PER:(b + 1) * PER], idf[:, b * PER:(b + 1) * PER],
                                                 float(b * ROWS), None, ALU.add))
                dve.wait_ge(m["all"], 1)
                link(nc.vector.tensor_scalar(keep["alpha"][:, 0:4], allp[:, :], 1e-30, 1.0 / SPAN, ALU.max, ALU.mult))
                nc.vector.reciprocal(unit[:, :], keep["alpha"][:, 0:4]).then_inc(m["unit"], 1)
                dve.wait_ge(m["unit"], 1)
                for n, i in enumerate((3, 2, 0, 1)):
                    (hi, lo), f = pairs[i]
                    link(nc.vector.tensor_scalar(f[:, :], f[:, :], unit[:, i:i + 1], None, ALU.mult))
                    link(nc.vector.tensor_copy(flat(hi[:]), f[:, :]))
                    nc.vector.tensor_tensor(flat(lo[:]), f[:, :], flat(hi[:]), ALU.subtract).then_inc(m["split_lo"], 1)
                for t in range(NT):
                    if t % XG == 0:
                        dve.wait_ge(x_loaded[t // XG % 2], 16 * (t // XG // 2 + 1))
                    nc.vector.bn_stats(stats[:, t, :], xg[:, t // XG % 2, t % XG, :]).then_inc(m["stat"], 1)
                    if t == XG:
                        dve.wait_ge(m["v_out"], 2 * B)
                        for i in range(2 * B):
                            rows = P if i % 2 == 0 else TAIL
                            last = nc.vector.tensor_reduce(vcol[0:rows, i:i + 1], kv[0:rows, i, D:2 * D], AX.X, ALU.max,
                                                           apply_absolute_value=True)
                        link(last)
                        nc.vector.tensor_reduce(vred[:, :], vcol[:, :], AX.X, ALU.max).then_inc(m["v_peak"], 1)
                dve.wait_ge(m["stat"], NT)
                for t in range(NT):
                    last = nc.vector.bn_aggr(mv[:, t, :], stats[:, t, :])
                link(last)
                nc.vector.tensor_scalar(veps[:, :], mv[:, :, 1], EPS, None, ALU.add).then_inc(m["veps"], 1)
                dve.wait_ge(m["v_all"], 1)
                link(nc.vector.tensor_scalar(vinv[:, :], vall[:, :], 1e-30, 1.0 / VSPAN, ALU.max, ALU.mult))
                nc.vector.tensor_copy(keep["alpha"][:, 7:8], vinv[:, :])
                link(nc.vector.reciprocal(unit[:, 0:1], vinv[:, :]))
                dve.wait_ge(m["k_out"], 2 * B)
                for i in range(2 * B):
                    rows = P if i % 2 == 0 else TAIL
                    last = nc.vector.tensor_scalar(kv[0:rows, i, D:2 * D], kv[0:rows, i, D:2 * D], unit[0:rows, 0:1], None, ALU.mult)
                last.then_inc(m["v_scaled"], 1)
                dve.wait_ge(m["ln"], 2)
                link(nc.vector.tensor_tensor(y1[:, :], y0[:, :], y0[:, :], ALU.mult))
                link(nc.vector.tensor_tensor(y2[:, :], y1[:, :], veps[:, :], ALU.mult))
                link(nc.vector.tensor_scalar(y1[:, :], y2[:, :], -0.5, 1.5, ALU.mult, ALU.add))
                link(nc.vector.tensor_tensor(keep["rstd"][:, :], y0[:, :], y1[:, :], ALU.mult))
                link(nc.vector.scalar_tensor_tensor(out=keep["shift"][:, :], in0=mv[:, :, 0], scalar=-1.0,
                                                    in1=keep["rstd"][:, :], op0=ALU.mult, op1=ALU.mult))
                al = keep["alpha"]
                link(nc.vector.tensor_tensor(al[:, 8:9], al[:, 2:3], al[:, 3:4], ALU.mult))
                link(nc.vector.tensor_scalar(al[:, 9:10], al[:, 8:9], al[:, 0:1], float(HD) ** -0.5, ALU.mult, ALU.mult))
                link(nc.vector.tensor_scalar(al[:, 10:11], al[:, 8:9], al[:, 1:2], al[:, 7:8], ALU.mult, ALU.mult))

            @block.scalar
            def _(act):
                for i in range(2 * B):
                    rows = P if i % 2 == 0 else TAIL
                    for half in range(2):
                        n = 2 * i + half
                        act.wait_ge(m["kv_ready"], n + 1)
                        nc.scalar.activation(kv[0:rows, i, half * D:(half + 1) * D], pk[n % 8][0:rows, :],
                                             ACT.Copy).then_inc(m["v_out" if half else "k_out"], 1)
                act.wait_ge(m["veps"], 1)
                nc.scalar.activation(lnv[:, :], veps[:, :], ACT.Ln).then_inc(m["ln"], 1)
                act.wait_ge(m["ln"], 1)
                nc.scalar.activation(y0[:, :], lnv[:, :], ACT.Exp, scale=-0.5).then_inc(m["ln"], 1)

            @block.gpsimd
            def _(pool):
                pool.wait_ge(m["peaks"], 1)
                nc.gpsimd.partition_all_reduce(allp[:, :], peaks[:, :], P, PEAK).then_inc(m["all"], 1)
                pool.wait_ge(m["v_peak"], 1)
                nc.gpsimd.partition_all_reduce(vall[:, :], vred[:, :], P, PEAK).then_inc(m["v_all"], 1)

            @block.tensor
            def _(pe):
                pe.wait_ge(m["split_lo"], 2)
                for i in range(2 * B):
                    b, r0, rows = i // 2, (0, P)[i % 2], (P, TAIL)[i % 2]
                    for half in range(2):
                        n = 2 * i + half
                        if n >= 8:
                            pe.wait_ge(m["v_out" if half else "k_out"], (n - 8) // 2 + 1)
                        todo = [(a, w, c) for c in range(DC) for a, w in ((0, 0), (0, 1), (1, 0))]
                        for q, (a, w, c) in enumerate(todo):
                            mm = nc.tensor.matmul(pk[n % 8][0:rows, :], cx[a][:, c, b, r0:r0 + rows],
                                                  kv_w[w][:, c, half * D:(half + 1) * D],
                                                  start=(q == 0), stop=(q == len(todo) - 1))
                        mm.then_inc(m["kv_ready"], 1)


def prepare_quant(nc, keep, gate_n, up_n, down_n):
    NB = FC * D // QB
    with Scope(nc, "pq") as s:
        nat = s.sb("nat", [P, 2, FC * D], F32)
        q16 = s.sb("q16", [P, FC * D], I16)
        nhi, nlo = (s.sb(n, [P, FC * D], F16) for n in ("nhi", "nlo"))
        peak, sc, rs, su = (s.sb(n, [P, NB], F32) for n in ("peak", "sc", "rs", "su"))
        red, allm, unit = (s.sb(n, [P, 1], F32) for n in ("red", "allm", "unit_w"))
        pt = [s.ps(f"pt{i}", [P, 4 * P], F16) for i in range(4)]
        loaded = [s.sem(f"loaded{i}") for i in range(3)]
        m = s.sems("red all dve scaled hi lo turned out")
        mats = [(gate_n, keep["gate"], 4), (up_n, keep["up"], 5), (down_n, keep["down"], 6)]

        with nc.Block() as block:
            @block.sync
            def _(sp):
                for i, (src, _, _) in enumerate(mats):
                    need(sp, m["lo"], i - 1)
                    sp.dma_start(nat[:, i % 2, :], src).then_inc(loaded[i], 16)

            @block.vector
            def _(dve):
                link = chain(dve, m["dve"])
                for i, (_, _, a) in enumerate(mats):
                    w = nat[:, i % 2, :].rearrange("p (n k) -> p n k", k=QB)
                    q = q16[:, :].rearrange("p (n k) -> p n k", k=QB)

                    def wide(t):
                        return t[:, :].unsqueeze(2).to_broadcast([P, NB, QB])
                    dve.wait_ge(loaded[i], 16)
                    link(nc.vector.tensor_reduce(peak[:, :], w, AX.X, ALU.max, apply_absolute_value=True))
                    link(nc.vector.tensor_scalar(sc[:, :], peak[:, :], 1.0 / WMAX, TINY, ALU.mult, ALU.max))
                    link(nc.vector.reciprocal(rs[:, :], sc[:, :]))
                    link(nc.vector.tensor_tensor(q, w, wide(rs), ALU.mult))
                    nc.vector.tensor_reduce(red[:, :], sc[:, :], AX.X, ALU.max).then_inc(m["red"], 1)
                    dve.wait_ge(m["all"], i + 1)
                    link(nc.vector.tensor_scalar(keep["alpha"][:, a:a + 1], allm[:, :], WMAX / SPAN, None, ALU.mult))
                    link(nc.vector.reciprocal(unit[:, :], keep["alpha"][:, a:a + 1]))
                    link(nc.vector.tensor_scalar(su[:, :], sc[:, :], unit[:, 0:1], None, ALU.mult))
                    nc.vector.tensor_tensor(w, q, wide(su), ALU.mult).then_inc(m["scaled"], 1)
                    dve.wait_ge(m["hi"], i + 1)
                    need(dve, m["turned"], 12 * i * 2)
                    nc.vector.tensor_tensor(nlo[:, :], nat[:, i % 2, :], nhi[:, :], ALU.subtract).then_inc(m["lo"], 1)

            @block.scalar
            def _(act):
                for i, (_, dst, _) in enumerate(mats):
                    act.wait_ge(m["scaled"], i + 1)
                    need(act, m["turned"], 12 * i * 2)
                    nc.scalar.activation(nhi[:, :], nat[:, i % 2, :], ACT.Copy).then_inc(m["hi"], 1)
                    for g in range(24):
                        part, r = g // 12, g % 12
                        act.wait_ge(m["turned"], 24 * i + g + 1)
                        out = dst[part][:, :, r * P:(r + 1) * P] if i < 2 else dst[part][:, r, :]
                        src = pt[g % 4][:, :].rearrange("p (c n) -> p c n", c=4) if i < 2 else pt[g % 4][:, :]
                        nc.scalar.activation(out, src, ACT.Copy).then_inc(m["out"], 1)

            @block.gpsimd
            def _(pool):
                for i in range(3):
                    pool.wait_ge(m["red"], i + 1)
                    nc.gpsimd.partition_all_reduce(allm[:, :], red[:, :], P, PEAK).then_inc(m["all"], 1)

            @block.tensor
            def _(pe):
                for i in range(3):
                    for g in range(24):
                        part, r = g // 12, g % 12
                        if r == 0:
                            pe.wait_ge(m["lo" if part else "hi"], i + 1)
                        need(pe, m["out"], 24 * i + g - 3)
                        src = (nlo if part else nhi)[:, :]
                        for c in range(4):
                            at = r * D + c * P if i < 2 else c * F + r * P
                            mm = nc.tensor.transpose(pt[g % 4][:, c * P:(c + 1) * P], src[:, at:at + P], keep["ident16"][:, :])
                        mm.then_inc(m["turned"], 1)


def attention(nc, keep, x, table, x1_d, hT_d, B):
    T = x.shape[0]
    NT = T // P
    U = 8
    KR = 4
    with Scope(nc, "at") as s:
        xs = s.sb("xs", [P, U, D], F32)
        kv = s.sb("kv_rows", [P, KR, W, 2 * D], F32)
        xn, att, hn = (s.sb(n, [P, 2, D], F32) for n in ("xn", "att", "hn"))
        xhi, xlo, ahi, alo = (s.sb(n, [P, 2, DC, P], F16) for n in ("xhi", "xlo", "ahi", "alo"))
        hT = s.sb("hT", [P, 4, D], F32)
        raw, sc, ds, ex, pr = (s.sb(n, [P, W, H], F32) for n in ("raw", "sc", "ds", "ex", "pr"))
        top, tot, inv = (s.sb(n, [P, H], F32) for n in ("top", "tot", "inv"))
        stats, mv = s.sb("stats2", [P, 6], F32), s.sb("mv2", [P, 2, 2], F32)
        veps, mr = s.sb("veps2", [P, 1], F32), s.sb("mr", [P, 1], F32)
        rstd, shift = s.sb("rstd2", [P, 2], F32), s.sb("shift2", [P, 2], F32)
        eps, expo, zero = (s.sb(n, [P, 1], F32) for n in ("eps", "expo", "zero"))
        psX, psA = s.ps("psX", [P, DC, P]), s.ps("psA", [P, DC, P])
        psQ = [s.ps(f"psQ{i}", [P, D]) for i in range(2)]
        psO = [s.ps(f"psO{i}", [P, D]) for i in range(2)]
        psH = [s.ps(f"psH{i}", [P, DC, P]) for i in range(2)]
        x_in, x1_out, hT_out = Transfers(s, "x_in", U), Transfers(s, "x1_out", U), Transfers(s, "hT_out", 4)
        rows_in = Transfers(s, "rows_in", KR, 16 * W)
        m = s.sems("xn xT xhi xlo q prod raw sc top ds ex tot inv pr pv half att aT ahi alo o x1 "
                         "stats mv veps rstd mr norm hn hT hT_sb peak consts")
        wq, wo, ident = keep["wq"], keep["wo"], keep["ident32"]
        x_v = x.rearrange("(n p) d -> p n d", p=P)

        with nc.Block() as block:
            @block.sync
            def _(sp):
                def tick(c):
                    at, live, u = c.at, c.live, c.u
                    if live(5):
                        if u == 0:
                            x1_out.done(sp, c, -3)
                            need(sp, m["hn"], at(-2))
                        else:
                            need(sp, m["hn"], at(-2))
                            x1_out.done(sp, c, -3)
                        sp.dma_start(xs[:, (u + 5) % U, :], x_v[:, bass.ds(at(5), 1), :]).then_inc(x_in.of(c, 5), 16)
                    if live(-1):
                        need(sp, m["x1"], at(0))
                        sp.dma_start(x1_d[bass.ds(at(-1), 1), :, :].rearrange("a p d -> p (a d)"), xs[:, (u - 1) % U, :]).then_inc(x1_out.of(c, -1), 16)
                    if live(-3):
                        need(sp, m["hT_sb"], at(-2))
                        sp.dma_start(hT_d[bass.ds(at(-3), 1)].rearrange("a p d -> p (a d)"), hT[:, (u - 3) % 4, :]).then_inc(hT_out.of(c, -3), 16)
                pipeline(sp, tick, NT, U, before=5, after=3)
                x1_out.all_done(sp, NT)
                hT_out.all_done(sp, NT)

            @block.scalar
            def _(act):
                def tick(c):
                    at, live, u = c.at, c.live, c.u
                    if live(-2):
                        need(act, m["norm"], at(-1))
                        need(act, m["hT"], at(-3))
                        nc.scalar.activation(hn[:, (u - 2) % 2, :], xs[:, (u - 2) % U, :], ACT.Identity,
                                             bias=shift[:, u % 2:u % 2 + 1],
                                             scale=rstd[:, u % 2:u % 2 + 1]).then_inc(m["hn"], 1)
                    if live(2):
                        need(act, m["xT"], at(3))
                        need(act, m["q"], at(1))
                        nc.scalar.activation(xhi[:, u % 2], psX[:, :, :], ACT.Copy).then_inc(m["xhi"], 1)
                    if live(-1):
                        need(act, m["aT"], at(0))
                        need(act, m["o"], at(-2))
                        nc.scalar.activation(ahi[:, (u - 1) % 2], psA[:, :, :], ACT.Copy).then_inc(m["ahi"], 1)
                    if live(0):
                        need(act, m["ds"], at(1))
                        need(act, m["pr"], at(0))
                        nc.scalar.activation(ex[:, :, :], ds[:, :, :], ACT.Exp).then_inc(m["ex"], 1)
                    if live(3):
                        x_in.done(act, c, 3)
                        need(act, m["xT"], at(2))
                        nc.scalar.activation(xn[:, (u + 3) % 2, :], xs[:, (u + 3) % U, :], ACT.Identity,
                                             bias=keep["shift"][:, bass.ds(at(3), 1)],
                                             scale=keep["rstd"][:, bass.ds(at(3), 1)]).then_inc(m["xn"], 1)
                    if live(-2):
                        need(act, m["hT"], at(-1))
                        hT_out.done(act, c, -6)
                        need(act, m["peak"], at(-5))
                        nc.scalar.activation(hT[:, (u - 2) % 4, :], psH[u % 2][:, :, :].rearrange("p c t -> p (c t)"),
                                             ACT.Copy).then_inc(m["hT_sb"], 1)
                pipeline(act, tick, NT, U, before=3, after=2)

            @block.vector
            def _(dve):
                nc.vector.memset(eps[:, :], EPS)
                nc.vector.memset(expo[:, :], -0.5)
                nc.vector.memset(zero[:, :], 0.0).then_inc(m["consts"], 1)

                def tick(c):
                    at, live, u = c.at, c.live, c.u
                    if live(0):
                        keys = kv[:, u % KR, :, 0:D]
                        rows_in.done(dve, c)
                        need(dve, m["q"], at(1))
                        nc.vector.tensor_tensor(keys, keys, psQ[u % 2][:, :].unsqueeze(1).to_broadcast([P, W, D]),
                                                ALU.mult).then_inc(m["prod"], 1)
                        need(dve, m["prod"], at(1))
                        nc.vector.tensor_reduce(raw[:, :, :],
                                                keys.rearrange("p w (h e) -> p w h e", h=H),
                                                AX.X, ALU.add).then_inc(m["raw"], 1)
                        need(dve, m["raw"], at(1))
                        nc.vector.scalar_tensor_tensor(
                            out=sc[:, :, :], in0=raw[:, :, :], scalar=keep["alpha"][:, 9:10],
                            in1=keep["mask"][:, bass.ds(at(0), 1), :].rearrange("p a w -> p (a w)").unsqueeze(2).to_broadcast([P, W, H]),
                            op0=ALU.mult, op1=ALU.add).then_inc(m["sc"], 1)
                        need(dve, m["sc"], at(1))
                        nc.vector.tensor_reduce(top[:, :], sc[:, :, :].rearrange("p w h -> p h w"), AX.X,
                                                ALU.max).then_inc(m["top"], 1)
                        need(dve, m["top"], at(1))
                        nc.vector.tensor_tensor(ds[:, :, :], sc[:, :, :], top[:, :].unsqueeze(1).to_broadcast([P, W, H]),
                                                ALU.subtract).then_inc(m["ds"], 1)
                    if live(-1):
                        need(dve, m["ahi"], at(0))
                        nc.vector.tensor_tensor(alo[:, (u - 1) % 2], psA[:, :, :], ahi[:, (u - 1) % 2],
                                                ALU.subtract).then_inc(m["alo"], 1)
                    if live(2):
                        need(dve, m["xhi"], at(3))
                        nc.vector.tensor_tensor(xlo[:, u % 2], psX[:, :, :], xhi[:, u % 2],
                                                ALU.subtract).then_inc(m["xlo"], 1)
                    if live(0):
                        need(dve, m["ex"], at(1))
                        nc.vector.tensor_reduce(tot[:, :], ex[:, :, :].rearrange("p w h -> p h w"), AX.X,
                                                ALU.add).then_inc(m["tot"], 1)
                        need(dve, m["tot"], at(1))
                        nc.vector.reciprocal(inv[:, :], tot[:, :]).then_inc(m["inv"], 1)
                        need(dve, m["inv"], at(1))
                        nc.vector.tensor_tensor(pr[:, :, :], ex[:, :, :], inv[:, :].unsqueeze(1).to_broadcast([P, W, H]),
                                                ALU.mult).then_inc(m["pr"], 1)
                        need(dve, m["pr"], at(1))
                        values = kv[:, u % KR, :, D:2 * D].rearrange("p w (h e) -> p w h e", h=H)
                        nc.vector.tensor_tensor(values, values, pr[:, :, :].unsqueeze(3).to_broadcast([P, W, H, HD]),
                                                ALU.mult).then_inc(m["pv"], 1)
                    if live(-1):
                        need(dve, m["o"], at(0))
                        nc.vector.scalar_tensor_tensor(out=xs[:, (u - 1) % U, :], in0=psO[(u - 1) % 2][:, :],
                                                       scalar=keep["alpha"][:, 10:11], in1=xs[:, (u - 1) % U, :],
                                                       op0=ALU.mult, op1=ALU.add).then_inc(m["x1"], 1)
                        need(dve, m["x1"], at(0))
                        nc.vector.bn_stats(stats[:, :], xs[:, (u - 1) % U, :]).then_inc(m["stats"], 1)
                        need(dve, m["stats"], at(0))
                        need(dve, m["norm"], at(-2))
                    if live(-3):
                        need(dve, m["hT_sb"], at(-2))
                        nc.vector.tensor_reduce(keep["h_peak"][:, bass.ds(at(-3), 1)], hT[:, (u - 3) % 4, :],
                                                AX.X, ALU.max, apply_absolute_value=True).then_inc(m["peak"], 1)
                    if live(-1):
                        nc.vector.bn_aggr(mv[:, (u - 1) % 2, :], stats[:, :]).then_inc(m["mv"], 1)
                pipeline(dve, tick, NT, U, before=2, after=3)

            @block.gpsimd
            def _(pool):
                def gather(t):
                    if t < NT:
                        for j in range(W):
                            pool.indirect_dma_start(out=kv[:, t % KR, j, :], out_offset=None, in_=table,
                                                    in_offset=bass.IndirectOffsetOnAxis(ap=keep["rows"][:, t:t + 1], axis=0),
                                                    element_offset=j * 2 * D).then_inc(rows_in.sems[t % KR], 16)

                def norm(t):
                    if t < 0:
                        return
                    k = t % 2
                    pool.wait_ge(m["mv"], t + 1)
                    nc.gpsimd.tensor_tensor(veps[:, :], mv[:, k, 1:2], eps[:, :], ALU.add).then_inc(m["veps"], 1)
                    pool.wait_ge(m["veps"], t + 1)
                    need(pool, m["hn"], t - 1)
                    nc.gpsimd.tensor_tensor(rstd[:, k:k + 1], veps[:, :], expo[:, :], ALU.pow).then_inc(m["rstd"], 1)
                    pool.wait_ge(m["rstd"], t + 1)
                    nc.gpsimd.tensor_tensor(mr[:, :], mv[:, k, 0:1], rstd[:, k:k + 1], ALU.mult).then_inc(m["mr"], 1)
                    pool.wait_ge(m["mr"], t + 1)
                    nc.gpsimd.tensor_tensor(shift[:, k:k + 1], zero[:, :], mr[:, :], ALU.subtract).then_inc(m["norm"], 1)

                pool.wait_ge(m["consts"], 1)
                for t in range(KR):
                    gather(t)
                for t in range(NT):
                    lower, upper = kv[:, t % KR, 0:2, D:2 * D], kv[:, t % KR, 2:4, D:2 * D]
                    pool.wait_ge(m["pv"], t + 1)
                    nc.gpsimd.tensor_tensor(lower, lower, upper, ALU.add).then_inc(m["half"], 1)
                    pool.wait_ge(m["half"], t + 1)
                    need(pool, m["aT"], t - 1)
                    nc.gpsimd.tensor_tensor(att[:, t % 2, :], kv[:, t % KR, 0, D:2 * D], kv[:, t % KR, 1, D:2 * D],
                                            ALU.add).then_inc(m["att"], 1)
                    norm(t - 1)
                    pool.wait_ge(m["att"], t + 1)
                    gather(t + KR)
                norm(NT - 1)

            @block.tensor
            def _(pe):
                def project(out, hi, lo, w, slot):
                    todo = [(a, b, c) for c in range(DC) for a, b in ((hi, 0), (hi, 1), (lo, 0))]
                    for q, (a, b, c) in enumerate(todo):
                        mm = nc.tensor.matmul(out[:, :], a[:, slot, c, :], w[b][:, c, :],
                                              start=(q == 0), stop=(q == len(todo) - 1))
                    return mm

                def turn(out, a):
                    for c in range(DC):
                        mm = nc.tensor.transpose(out[:, c, :], a[:, c * P:(c + 1) * P], ident[:, :])
                    return mm

                def tick(c):
                    at, live, u = c.at, c.live, c.u
                    if live(2):
                        need(pe, m["xn"], at(3))
                        need(pe, m["xlo"], at(2))
                        turn(psX, xn[:, u % 2, :]).then_inc(m["xT"], 1)
                    if live(1):
                        need(pe, m["xlo"], at(2))
                        need(pe, m["prod"], at(0))
                        project(psQ[(u + 1) % 2], xhi, xlo, wq, (u + 1) % 2).then_inc(m["q"], 1)
                    if live(-1):
                        need(pe, m["att"], at(0))
                        need(pe, m["alo"], at(-1))
                        turn(psA, att[:, (u - 1) % 2, :]).then_inc(m["aT"], 1)
                    if live(-2):
                        need(pe, m["hn"], at(-1))
                        need(pe, m["hT_sb"], at(-3))
                        turn(psH[u % 2], hn[:, u % 2, :]).then_inc(m["hT"], 1)
                    if live(-1):
                        need(pe, m["alo"], at(0))
                        need(pe, m["x1"], at(-2))
                        project(psO[(u - 1) % 2], ahi, alo, wo, (u - 1) % 2).then_inc(m["o"], 1)
                pipeline(pe, tick, NT, U, before=2, after=2)


def whole_peak(nc, s, m, name, cols):
    red, out = s.sb(f"{name}_red", [P, 1], F32), s.sb(f"{name}_all", [P, 1], F32)

    def on_vector(dve):
        nc.vector.tensor_reduce(red[:, :], cols, AX.X, ALU.max).then_inc(m[f"{name}_red"], 1)

    def on_pool(pool):
        pool.wait_ge(m[f"{name}_red"], 1)
        nc.gpsimd.partition_all_reduce(out[:, :], red[:, :], P, PEAK).then_inc(m[f"{name}_all"], 1)
    return out, on_vector, on_pool


def quantiser(nc, link, scale, inv, peak, unit):
    link(nc.vector.tensor_scalar(scale, peak, unit, 1.0 / QMAX, ALU.mult, ALU.mult))
    link(nc.vector.tensor_scalar(scale, scale, TINY, None, ALU.max))
    link(nc.vector.reciprocal(inv, scale))
    link(nc.vector.tensor_tensor(inv, inv, unit, ALU.mult))


def feed_in(nc, keep, hT_d, raw_d, NB, gate_d=None):
    up = gate_d is not None
    name = "up" if up else "ga"
    wt = keep["up" if up else "gate"]
    g = keep["g"]
    U = 2
    PAIRS = FC // 2
    with Scope(nc, name) as s:
        hT_v = hT_d.rearrange("(b n) p d -> b p n d", n=SUB)
        hb = s.sb("hb", [P, 2, SUB, D], F32)
        hq = s.sb("hq", [P, DC * BLK], I16)
        ah, al = (s.sb(n, [P, 2, SUB, DC, P], F16) for n in ("ah", "al"))
        raw = s.sb("raw", [P, 3, UE], F32)
        pp = [s.ps(f"pp{i}", [P, 2, BLK]) for i in range(4)]
        h_in, stored = Transfers(s, "h_in", 2), Transfers(s, "stored", UNITS)
        gate_in, gate_out = Transfers(s, "gate_in", 3), Transfers(s, "gate_out", 2)
        m = s.sems("h_red h_all g_red g_all dve scales hq ah al mm out peak gq sig sq prod gpeak")
        if up:
            gin, gp = s.sb("gin", [P, 3, UE], F32), s.sb("gp", [P, 2, UE], F32)
            sig = s.sb("sig", [P, 2, UE], F32)
            gq, sq = s.sb("gq", [P, 2, UE], I16), s.sb("sq", [P, 2, UE], U16)
            gate_u = gate_d.rearrange("b q p d -> (b q) p d")
            peak, peak_v, peak_p = whole_peak(nc, s, m, "g", keep["gate_peak"][:, :])
        else:
            peak, peak_v, peak_p = whole_peak(nc, s, m, "h", keep["h_peak"][:, :])
            gate_u = None
        out_peak = keep["up_peak" if up else "gate_peak"]

        with nc.Block() as block:
            @block.sync
            def _(sp):
                def tick(c):
                    at, live, u = c.at, c.live, c.u
                    if live(2):
                        need(sp, m["hq"], at(1))
                        sp.dma_start(hb[:, u % 2], hT_v[bass.ds(at(2), 1)].rearrange("a p n d -> p (a n) d")).then_inc(h_in.of(c, 2), 16)
                    for q in range(UNITS):
                        n = at(0) * UNITS + q
                        if up and c.live_unit(UNITS, q + 3):
                            need(sp, m["gq"], n + 1)
                            sp.dma_start(gin[:, q, :], gate_u[bass.ds(n + 3, 1)].rearrange("a p d -> p (a d)")).then_inc(gate_in.of(c, 0, UNITS, q + 3), 16)
                        if up and c.live_unit(UNITS, q + 1):
                            need(sp, m["gpeak"], n + 2)
                            sp.dma_start(gate_u[bass.ds(n + 1, 1)].rearrange("a p d -> p (a d)"),
                                         gp[:, (u * UNITS + q + 1) % 2, :]).then_inc(gate_out.of(c, 0, UNITS, q + 1), 16)
                        if live(0):
                            need(sp, m["peak"], n + 1)
                            sp.dma_start(raw_d[bass.ds(at(0), 1), q].rearrange("a p d -> p (a d)"), raw[:, q, :]).then_inc(stored.of(c, 0, UNITS, q), 16)
                pipeline(sp, tick, NB, U, before=2)
                stored.all_done(sp, UNITS * NB)
                if up:
                    gate_out.all_done(sp, UNITS * NB)

            @block.gpsimd
            def _(pool):
                peak_p(pool)

            @block.vector
            def _(dve):
                link = chain(dve, m["dve"])
                peak_v(dve)
                if not up:
                    dve.wait_ge(m["h_all"], 1)
                    link(nc.vector.memset(g[:, 15:16], 1.0))
                    quantiser(nc, link, g[:, 0:1], g[:, 1:2], peak[:, :], g[:, 15:16])
                    link(nc.vector.tensor_tensor(g[:, 2:3], g[:, 0:1], keep["alpha"][:, 4:5], ALU.mult))
                    link(nc.vector.tensor_tensor(g[:, 3:4], g[:, 0:1], keep["alpha"][:, 5:6], ALU.mult))
                else:
                    dve.wait_ge(m["g_all"], 1)
                    quantiser(nc, link, g[:, 4:5], g[:, 5:6], peak[:, :], g[:, 2:3])
                nc.vector.memset(g[:, 14:15], 0.0).then_inc(m["scales"], 1)

                def tick(c):
                    at, live, u = c.at, c.live, c.u
                    if live(1):
                        a = (u + 1) % 2
                        need(dve, m["hq"], at(2))
                        need(dve, m["mm"], at(0) * PAIRS)
                        nc.vector.tensor_copy(ah[:, a].rearrange("p n c t -> p (n c t)"), hq[:, :]).then_inc(m["ah"], 1)
                        need(dve, m["ah"], at(2))
                        nc.vector.tensor_tensor(al[:, a].rearrange("p n c t -> p (n c t)"), hq[:, :],
                                                ah[:, a].rearrange("p n c t -> p (n c t)"), ALU.subtract).then_inc(m["al"], 1)
                    for q in range(UNITS):
                        n = at(0) * UNITS + q
                        if up and c.live_unit(UNITS, q + 1):
                            k = (u * UNITS + q + 1) % 2
                            need(dve, m["sig"], n + 2)
                            need(dve, m["prod"], n)
                            nc.vector.tensor_scalar(sq[:, k, :], sig[:, k, :], 65536.0, 65535.0, ALU.mult, ALU.min).then_inc(m["sq"], 1)
                            need(dve, m["sq"], n + 2)
                            gate_out.done(dve, c, 0, UNITS, q - 1)
                            nc.vector.tensor_tensor(gp[:, k, :], gq[:, k, :], sq[:, k, :], ALU.mult).then_inc(m["prod"], 1)
                            need(dve, m["prod"], n + 2)
                            nc.vector.tensor_reduce(keep["gated_peak"][:, bass.ds(n + 1, 1)], gp[:, k, :], AX.X, ALU.max,
                                                    apply_absolute_value=True).then_inc(m["gpeak"], 1)
                        if live(0):
                            need(dve, m["out"], n * 2 + 2)
                            nc.vector.tensor_reduce(out_peak[:, bass.ds(n, 1)], raw[:, q, :], AX.X, ALU.max,
                                                    apply_absolute_value=True).then_inc(m["peak"], 1)
                pipeline(dve, tick, NB, U, before=1)

            @block.scalar
            def _(act):
                act.wait_ge(m["scales"], 1)

                def tick(c):
                    at, live, u = c.at, c.live, c.u
                    def quantise_next():
                        if live(1):
                            h_in.done(act, c, 1)
                            need(act, m["al"], at(1))
                            nc.scalar.activation(hq[:, :], hb[:, (u + 1) % 2].rearrange("p n d -> p (n d)"), ACT.Copy, scale=g[:, 1:2]).then_inc(m["hq"], 1)
                    if not live(0):
                        quantise_next()
                    for q in range(UNITS):
                        n = at(0) * UNITS + q
                        if up and c.live_unit(UNITS, q + 1):
                            k = (u * UNITS + q + 1) % 2
                            gate_in.done(act, c, 0, UNITS, q + 1)
                            need(act, m["prod"], n)
                            nc.scalar.activation(gq[:, k, :], gin[:, (q + 1) % 3, :], ACT.Copy, scale=g[:, 5:6]).then_inc(m["gq"], 1)
                            need(act, m["gq"], n + 2)
                            need(act, m["sq"], n)
                            nc.scalar.activation(sig[:, k, :], gq[:, k, :], ACT.Sigmoid, scale=g[:, 4:5]).then_inc(m["sig"], 1)
                        if not live(0):
                            continue
                        for h in range(2):
                            pair = 2 * q + h
                            need(act, m["mm"], at(0) * PAIRS + pair + 1)
                            if h == 0:
                                stored.done(act, c, 0, UNITS, q - UNITS)
                            nc.scalar.activation(raw[:, q, h * 2 * BLK:(h + 1) * 2 * BLK],
                                                 pp[(u * PAIRS + pair) % 4][:, :, :].rearrange("p a t -> p (a t)"),
                                                 ACT.Copy).then_inc(m["out"], 1)
                        if q == 0:
                            quantise_next()
                pipeline(act, tick, NB, U, before=1)

            @block.tensor
            def _(pe):
                def tick(c):
                    at, live, u = c.at, c.live, c.u
                    need(pe, m["al"], at(1))
                    for pair in range(PAIRS):
                        need(pe, m["out"], at(0) * PAIRS + pair - 3)
                        bank = pp[(u * PAIRS + pair) % 4]
                        for h in range(2):
                            f = (2 * pair + h) * P
                            todo = [(w, a, c) for c in range(DC) for w, a in ((0, ah), (0, al), (1, ah))]
                            for q, (w, a, c) in enumerate(todo):
                                mm = nc.tensor.matmul(bank[:, h, :], wt[w][:, c, f:f + P], a[:, u % 2, :, c, :],
                                                      start=(q == 0), stop=(q == len(todo) - 1))
                        mm.then_inc(m["mm"], 1)
                pipeline(pe, tick, NB, U)


def product_peak(nc, keep, gate_d, up_d, NB):
    g = keep["g"]
    N, U = NB * UNITS, 4
    gv, uv = (t.rearrange("b q p d -> (b q) p d") for t in (gate_d, up_d))
    with Scope(nc, "pp") as s:
        gi, ui = s.sb("gi", [P, 4, UE], F32), s.sb("ui", [P, 4, UE], F32)
        ga, ua = s.sb("ga", [P, 2, UE], I16), s.sb("ua", [P, 2, UE], I16)
        junk = s.sb("junk", [P, UE], F32)
        col = s.sb("col", [P, 4], F32)
        gin, uin = Transfers(s, "gin", 4), Transfers(s, "uin", 4)
        m = s.sems("g_red g_all u_red u_all dve scales ga ua prod col")
        pg, pg_v, pg_p = whole_peak(nc, s, m, "g", keep["gated_peak"][:, :])
        pu, pu_v, pu_p = whole_peak(nc, s, m, "u", keep["up_peak"][:, :])

        with nc.Block() as block:
            @block.sync
            def _(sp):
                def tick(c):
                    at, live, u = c.at, c.live, c.u
                    if live(3):
                        need(sp, m["ga"], at(0))
                        sp.dma_start(gi[:, (u + 3) % 4, :], gv[bass.ds(at(3), 1)].rearrange("a p d -> p (a d)")).then_inc(gin.of(c, 3), 16)
                        need(sp, m["ua"], at(0))
                        sp.dma_start(ui[:, (u + 3) % 4, :], uv[bass.ds(at(3), 1)].rearrange("a p d -> p (a d)")).then_inc(uin.of(c, 3), 16)
                pipeline(sp, tick, N, U, before=3)

            @block.gpsimd
            def _(pool):
                pg_p(pool)
                pu_p(pool)

            @block.scalar
            def _(act):
                act.wait_ge(m["scales"], 1)

                def tick(c):
                    at, live, u = c.at, c.live, c.u
                    gin.done(act, c)
                    need(act, m["prod"], at(-1))
                    nc.scalar.activation(ga[:, u % 2, :], gi[:, u % 4, :], ACT.Abs, scale=g[:, 7:8]).then_inc(m["ga"], 1)
                    uin.done(act, c)
                    nc.scalar.activation(ua[:, u % 2, :], ui[:, u % 4, :], ACT.Abs, scale=g[:, 10:11]).then_inc(m["ua"], 1)
                pipeline(act, tick, N, U)

            @block.vector
            def _(dve):
                link = chain(dve, m["dve"])
                pg_v(dve)
                pu_v(dve)
                link(nc.vector.tensor_scalar(g[:, 6:7], g[:, 4:5], 1.0 / 65536.0, None, ALU.mult))
                dve.wait_ge(m["g_all"], 1)
                quantiser(nc, link, g[:, 8:9], g[:, 7:8], pg[:, :], g[:, 6:7])
                dve.wait_ge(m["u_all"], 1)
                quantiser(nc, link, g[:, 9:10], g[:, 10:11], pu[:, :], g[:, 3:4])
                nc.vector.tensor_tensor(g[:, 11:12], g[:, 8:9], g[:, 9:10], ALU.mult).then_inc(m["scales"], 1)

                def tick(c):
                    at, live, u = c.at, c.live, c.u
                    if live(0):
                        need(dve, m["ua"], at(1))
                        need(dve, m["ga"], at(1))
                        need(dve, m["col"], at(-1))
                    if live(-1):
                        need(dve, m["prod"], at(0))
                        nc.vector.tensor_copy(keep["o_peak"][:, bass.ds(at(-1), 1)], col[:, (u - 1) % 4:(u - 1) % 4 + 1]).then_inc(m["col"], 1)
                    if live(0):
                        nc.vector.tensor_tensor_reduce(out=junk[:, :], in0=ga[:, u % 2, :], in1=ua[:, u % 2, :], scale=1.0,
                                                       scalar=0.0, op0=ALU.mult, op1=ALU.max,
                                                       accum_out=col[:, u % 4:u % 4 + 1]).then_inc(m["prod"], 1)
                pipeline(dve, tick, N, U, after=1)


def feed_out(nc, keep, gate_d, up_d, x1_d, out, NB):
    g = keep["g"]
    wt = keep["down"]
    U = 2
    out_v = out.rearrange("(b n p) d -> b p n d", p=P, n=SUB)
    x1_v = x1_d.rearrange("(b n) p d -> b p n d", n=SUB)
    gate_u, up_u = (d.rearrange("b q p d -> (b q) p d") for d in (gate_d, up_d))
    with Scope(nc, "fo") as s:
        gi, ui = s.sb("gi", [P, 3, UE], F32), s.sb("ui", [P, 3, UE], F32)
        gq, uq = (s.sb(n, [P, 2, UE], I16) for n in ("gq", "uq"))
        oq = s.sb("oq", [P, UE], I16)
        o = s.sb("o", [P, UE], F32)
        oh, ol = (s.sb(n, [P, 2, FC, BLK], F16) for n in ("oh", "ol"))
        xb = s.sb("xb", [P, 2, SUB, D], F32)
        py = [s.ps(f"py{i}", [P, D]) for i in range(8)]
        gin, uin = Transfers(s, "gin", 3), Transfers(s, "uin", 3)
        x_in, stored = Transfers(s, "x_in", 2), Transfers(s, "stored", 2)
        m = s.sems("o_red o_all dve scales gq uq o oq oh ol mm y")
        po, po_v, po_p = whole_peak(nc, s, m, "o", keep["o_peak"][:, :])

        with nc.Block() as block:
            @block.sync
            def _(sp):
                def tick(c):
                    at, live, u = c.at, c.live, c.u
                    for q in range(UNITS):
                        n = at(0) * UNITS + q
                        if c.live_unit(UNITS, q + 4):
                            k = (q + 4) % 3
                            need(sp, m["gq"], n + 2)
                            sp.dma_start(gi[:, k, :], gate_u[bass.ds(n + 4, 1)].rearrange("a p d -> p (a d)")).then_inc(gin.of(c, 0, UNITS, q + 4), 16)
                            need(sp, m["uq"], n + 2)
                            sp.dma_start(ui[:, k, :], up_u[bass.ds(n + 4, 1)].rearrange("a p d -> p (a d)")).then_inc(uin.of(c, 0, UNITS, q + 4), 16)
                    if live(-1):
                        need(sp, m["y"], at(0) * SUB)
                        sp.dma_start(out_v[bass.ds(at(-1), 1)].rearrange("a p n d -> p (a n) d"), xb[:, (u + 1) % 2]).then_inc(stored.of(c, -1), 16)
                    if live(1):
                        stored.done(sp, c, -1)
                        sp.dma_start(xb[:, (u + 1) % 2], x1_v[bass.ds(at(1), 1)].rearrange("a p n d -> p (a n) d")).then_inc(x_in.of(c, 1), 16)
                pipeline(sp, tick, NB, U, before=2, after=1)
                stored.all_done(sp, NB)

            @block.gpsimd
            def _(pool):
                po_p(pool)

            @block.scalar
            def _(act):
                act.wait_ge(m["scales"], 1)

                def tick(c):
                    at, live, u = c.at, c.live, c.u
                    for q in range(UNITS):
                        n = at(0) * UNITS + q
                        if c.live_unit(UNITS, q + 4):
                            k = (u * UNITS + q) % 2
                            gin.done(act, c, 0, UNITS, q + 4)
                            need(act, m["o"], n + 3)
                            nc.scalar.activation(gq[:, k, :], gi[:, (q + 4) % 3, :], ACT.Copy, scale=g[:, 7:8]).then_inc(m["gq"], 1)
                            uin.done(act, c, 0, UNITS, q + 4)
                            nc.scalar.activation(uq[:, k, :], ui[:, (q + 4) % 3, :], ACT.Copy, scale=g[:, 10:11]).then_inc(m["uq"], 1)
                        if c.live_unit(UNITS, q + 3):
                            need(act, m["o"], n + 4)
                            need(act, m["ol"], n + 3)
                            nc.scalar.activation(oq[:, :], o[:, :], ACT.Copy, scale=g[:, 13:14]).then_inc(m["oq"], 1)
                pipeline(act, tick, NB, U, before=2)

            @block.vector
            def _(dve):
                link = chain(dve, m["dve"])
                po_v(dve)
                dve.wait_ge(m["o_all"], 1)
                quantiser(nc, link, g[:, 12:13], g[:, 13:14], po[:, :], g[:, 11:12])
                nc.vector.tensor_tensor(g[:, 14:15], g[:, 12:13], keep["alpha"][:, 6:7], ALU.mult).then_inc(m["scales"], 1)
                dve.wait_ge(m["scales"], 1)

                def tick(c):
                    at, live, u = c.at, c.live, c.u

                    def sum_out(t):
                        n = at(0) * SUB + t
                        need(dve, m["mm"], n + 1)
                        if t == 0:
                            x_in.done(dve, c)
                        nc.vector.scalar_tensor_tensor(out=xb[:, u % 2, t, :], in0=py[(u * SUB + t) % 8][:, :],
                                                       scalar=g[:, 14:15], in1=xb[:, u % 2, t, :],
                                                       op0=ALU.mult, op1=ALU.add).then_inc(m["y"], 1)
                    for q in range(UNITS):
                        n = at(0) * UNITS + q
                        if c.live_unit(UNITS, q + 3):
                            f = (q + 3) % UNITS
                            b = (u + (q + 3) // UNITS) % 2
                            hi = oh[:, b, f * UN:(f + 1) * UN, :].rearrange("p f t -> p (f t)")
                            lo = ol[:, b, f * UN:(f + 1) * UN, :].rearrange("p f t -> p (f t)")
                            need(dve, m["oq"], n + 4)
                            if q == 0:
                                need(dve, m["mm"], at(0) * SUB)
                            nc.vector.tensor_copy(hi, oq[:, :]).then_inc(m["oh"], 1)
                        if c.live_unit(UNITS, q + 4):
                            k = (u * UNITS + q) % 2
                            need(dve, m["gq"], n + 5)
                            need(dve, m["uq"], n + 5)
                            need(dve, m["oq"], n + 4)
                            nc.vector.tensor_tensor(o[:, :], gq[:, k, :], uq[:, k, :], ALU.mult).then_inc(m["o"], 1)
                        if c.live_unit(UNITS, q + 3):
                            need(dve, m["oh"], n + 4)
                            nc.vector.tensor_tensor(lo, oq[:, :], hi, ALU.subtract).then_inc(m["ol"], 1)
                        if live(0):
                            sum_out(q)
                    if live(0):
                        sum_out(SUB - 1)
                pipeline(dve, tick, NB, U, before=2)

            @block.tensor
            def _(pe):
                def tick(c):
                    at, live, u = c.at, c.live, c.u
                    need(pe, m["ol"], at(1) * UNITS)
                    for t in range(SUB):
                        need(pe, m["y"], at(0) * SUB + t - 7)
                        todo = [(a, w, f) for f in range(FC) for a, w in ((oh, 0), (oh, 1), (ol, 0))]
                        for q, (a, w, f) in enumerate(todo):
                            mm = nc.tensor.matmul(py[(u * SUB + t) % 8][:, :], a[:, u % 2, f, t * P:(t + 1) * P],
                                                  wt[w][:, f, :], start=(q == 0), stop=(q == len(todo) - 1))
                        mm.then_inc(m["mm"], 1)
                pipeline(pe, tick, NB, U)


def identity(nc, keep):
    with Scope(nc, "id") as s:
        made = s.sem("made")
        with nc.Block() as block:
            @block.gpsimd
            def _(pool):
                nc.gpsimd.memset(keep["ident32"][:, :], 0.0).then_inc(made, 1)
                pool.wait_ge(made, 1)
                nc.gpsimd.affine_select(out=keep["ident32"][:, :], in_=keep["ident32"][:, :], compare_op=ALU.not_equal,
                                        fill=1.0, base=0, pattern=[[-1, P]], channel_multiplier=1).then_inc(made, 1)
                pool.wait_ge(made, 2)
                nc.gpsimd.tensor_copy(keep["ident16"][:, :], keep["ident32"][:, :]).then_inc(made, 1)
                pool.wait_ge(made, 3)


def build(nc, x, ctx_t, idx_t, wq_t, wkv_t, wo_t, gate_n, up_n, down_n, out, B, LKV):
    T = x.shape[0]
    NT, NB = T // P, T // BLK
    table = nc.dram_tensor("kv_table", [B * (LKV + 6), 2 * D], F32).ap()
    x1_d = nc.dram_tensor("x1_scratch", [NT, P, D], F32).ap()
    hT_d = nc.dram_tensor("hT_scratch", [NT, P, D], F32).ap()
    gate_d = nc.dram_tensor("gate_scratch", [NB, UNITS, P, UE], F32).ap()
    up_d = nc.dram_tensor("up_scratch", [NB, UNITS, P, UE], F32).ap()
    U3 = NB * UNITS
    with Scope(nc, "kept") as s:
        keep = {
            "down": [s.sb(f"down{i}", [P, FC, D], F16) for i in range(2)],
            "alpha": s.sb("alpha", [P, 12], F32),
            "g": s.sb("g", [P, 16], F32),
            "h_peak": s.sb("h_peak", [P, NT], F32), "gate_peak": s.sb("gate_peak", [P, U3], F32),
            "up_peak": s.sb("up_peak", [P, U3], F32), "gated_peak": s.sb("gated_peak", [P, U3], F32),
            "o_peak": s.sb("o_peak", [P, U3], F32),
        }
        with Scope(nc, "kept") as s_up:
            keep["up"] = [s_up.sb(f"up{i}", [P, DC, F], F16) for i in range(2)]
            with Scope(nc, "kept") as s_gate:
                keep["gate"] = [s_gate.sb(f"gate{i}", [P, DC, F], F16) for i in range(2)]
                with Scope(nc, "kept") as s_att:
                    for n in ("wq", "wo"):
                        keep[n] = [s_att.sb(f"{n}{i}", [P, DC, D], F16) for i in range(2)]
                    for n, shape, dt in (("ident32", [P, P], F32), ("ident16", [P, P], F16), ("rows", [P, NT], I32),
                                         ("mask", [P, NT, W], F32), ("rstd", [P, NT], F32), ("shift", [P, NT], F32)):
                        keep[n] = s_att.sb(n, shape, dt)
                    identity(nc, keep)
                    prepare_dense(nc, keep, x, ctx_t, idx_t, wq_t, wkv_t, wo_t, table, B, LKV)
                    prepare_quant(nc, keep, gate_n, up_n, down_n)
                    attention(nc, keep, x, table, x1_d, hT_d, B)
                feed_in(nc, keep, hT_d, gate_d, NB)
            feed_in(nc, keep, hT_d, up_d, NB, gate_d)
        product_peak(nc, keep, gate_d, up_d, NB)
        feed_out(nc, keep, gate_d, up_d, x1_d, out, NB)


def kernel(x, ctx_1024, itok_BxS_0_511, L0_xattn_Wq, L0_xattn_Wkv, L0_xattn_Wo, L0_ffn_w_gate, L0_ffn_w_up,
           L0_ffn_w_down):
    import numpy as np
    import concourse.bacc as bacc
    from concourse import mybir
    from concourse.bass_utils import run_bass_kernel_spmd

    B, LQ, _ = x.shape
    LKV = ctx_1024.shape[1]

    def contraction_first(w):
        w = np.asarray(w)
        return np.ascontiguousarray(w.T.reshape(DC, P, -1).transpose(1, 0, 2)).reshape(P, -1)

    def by_partition(w):
        w = np.asarray(w)
        return np.ascontiguousarray(w.reshape(-1, P, w.shape[1]).transpose(1, 0, 2)).reshape(P, -1)

    arrays = {
        "x": np.ascontiguousarray(np.asarray(x).reshape(B * LQ, D)),
        "ctx_t": contraction_first(np.asarray(ctx_1024).reshape(B * LKV, D)),
        "idx_t": np.ascontiguousarray(np.asarray(itok_BxS_0_511).reshape(-1, P).T),
        "wq_t": contraction_first(L0_xattn_Wq), "wkv_t": contraction_first(L0_xattn_Wkv),
        "wo_t": contraction_first(L0_xattn_Wo), "gate_n": by_partition(L0_ffn_w_gate),
        "up_n": by_partition(L0_ffn_w_up), "down_n": by_partition(L0_ffn_w_down),
    }
    nc = bacc.Bacc("TRN2", target_bir_lowering=False, num_devices=1)
    args = [nc.dram_tensor(f"in_{n}", a.shape, mybir.dt.from_np(a.dtype), kind="ExternalInput").ap()
            for n, a in arrays.items()]
    out = nc.dram_tensor("out", (B * LQ, D), mybir.dt.float32, kind="ExternalOutput").ap()
    build(nc, *args, out, B, LKV)
    r = run_bass_kernel_spmd(nc, [{f"in_{n}": a for n, a in arrays.items()}], core_ids=[0])
    return r.results[0]["out"].reshape(B, LQ, D)
```

```python
from contextlib import ExitStack

import concourse.bass as bass
from concourse import mybir

F32 = mybir.dt.float32
F16 = mybir.dt.float16
I16 = mybir.dt.int16
U16 = mybir.dt.uint16
I32 = mybir.dt.int32
ALU = mybir.AluOpType
ACT = mybir.ActivationFunctionType
AX = mybir.AxisListType
PEAK = bass.bass_isa.ReduceOp.max

P = 128
D = 512
DC = D // P
H, HD = 16, 32
W = 4
F = 1536
FC = F // P
QB = 32
BLK = 512
SUB = BLK // P
EPS = 1e-5
QMAX = 32767.0
WMAX = 7.0
TINY = 1e-12
SPAN = 1024.0
VSPAN = 64.0
LOW = -3.0e38
UN = 4
UNITS = FC // UN
UE = UN * BLK


def need(eng, sem, value):
    if isinstance(value, int) and value <= 0:
        return
    eng.wait_ge(sem, value)


class Tick:

    def __init__(self, n, unroll, u, k=None, s=None):
        self.n, self.unroll, self.u, self.k, self.s = n, unroll, u, k, s

    def at(self, off=0):
        return self.div(off, 1)

    def div(self, off, m, per=1, add=0):
        if self.k is None:
            return ((self.s + off) * per + add) // m
        assert self.unroll * per % m == 0
        return self.k * (self.unroll * per // m) + ((self.u + off) * per + add) // m

    def live(self, off=0):
        return self.k is not None or 0 <= self.s + off < self.n

    def first(self, off=0, per=1, add=0):
        return self.k is None and (self.s + off) * per + add == 0

    def live_unit(self, per, add):
        return self.k is not None or 0 <= self.s * per + add < self.n * per


def pipeline(eng, tick, n, unroll, before=0, after=0):
    assert n % unroll == 0 and n // unroll >= 3 and before <= unroll and after <= unroll
    for s in range(-before, unroll):
        tick(Tick(n, unroll, s % unroll, s=s))
    with eng.Fori(1, n // unroll - 1) as k:
        for u in range(unroll):
            tick(Tick(n, unroll, u, k=k))
    for s in range(n - unroll, n + after):
        tick(Tick(n, unroll, s % unroll, s=s))


class Transfers:

    def __init__(self, scope, name, slots, each=16):
        self.sems, self.slots, self.each = [scope.sem(f"{name}{i}") for i in range(slots)], slots, each

    def of(self, c, off=0, per=1, add=0):
        return self.sems[((c.u + off) * per + add) % self.slots]

    def done(self, eng, c, off=0, per=1, add=0):
        need(eng, self.of(c, off, per, add), self.each * (c.div(off, self.slots, per, add) + 1))

    def all_done(self, eng, n):
        for i, sem in enumerate(self.sems):
            need(eng, sem, self.each * ((n - i + self.slots - 1) // self.slots))


class Scope:

    def __init__(self, nc, tag):
        self.nc, self.tag, self.ctx, self.own = nc, tag, ExitStack(), []

    def __enter__(self):
        self.ctx.__enter__()
        return self

    def __exit__(self, *a):
        if self.own and a[0] is None:
            self.nc.clear_and_free_semaphores(self.own)
            self.nc.all_engine_barrier()
        return self.ctx.__exit__(*a)

    def sb(self, name, shape, dt):
        return self.ctx.enter_context(self.nc.sbuf_tensor(f"{self.tag}_{name}", shape, dt))

    def ps(self, name, shape, dt=F32):
        return self.ctx.enter_context(self.nc.psum_tensor(f"{self.tag}_{name}", shape, dt))

    def sem(self, name):
        self.own.append(self.nc.alloc_semaphore(f"{self.tag}_{name}"))
        return self.own[-1]

    def sems(self, names):
        return {n: self.sem(n) for n in names.split()}


def chain(eng, sem):
    count = [0]

    def link(ins):
        count[0] += 1
        ins.then_inc(sem, 1)
        eng.wait_ge(sem, count[0])
    return link


def prepare_dense(nc, keep, early, x, wq_t, wo_t, table, B, LKV):
    T = x.shape[0]
    NT = T // P
    PER = NT // B
    ROWS = LKV + 6
    TAIL = LKV - P
    XG, XB = 2, 4
    with Scope(nc, "pd") as s:
        fq, fo = s.sb("fq", [P, DC * D], F32), s.sb("fo", [P, DC * D], F32)
        kv_w = [s.sb(f"kv_w{i}", [P, DC, 2 * D], F16) for i in range(2)]
        cx = [s.sb(f"cx{i}", [P, DC, B, LKV], F16) for i in range(2)]
        kv = s.sb("kv", [P, 2 * B, 2 * D], F32)
        xg = early["wkv"][:, :].rearrange("p (b g d) -> p b g d", b=XB, g=XG)
        peaks, allp, unit = s.sb("peaks", [P, 4], F32), s.sb("allp", [P, 4], F32), s.sb("unit", [P, 4], F32)
        vcol, vred, vall, vinv = (s.sb(n, [P, m], F32) for n, m in (("vcol", 2 * B), ("vred", 1), ("vall", 1), ("vinv", 1)))
        stats, mv = s.sb("stats", [P, NT, 6], F32), s.sb("mv", [P, NT, 2], F32)
        veps, lnv, y0, y1, y2 = (s.sb(n, [P, NT], F32) for n in ("veps", "lnv", "y0", "y1", "y2"))
        idf = s.sb("idf", [P, NT], F32)
        pk = [s.ps(f"pk{i}", [P, D]) for i in range(8)]
        m = s.sems("peaks all unit split_lo kv_ready k_out v_out v_peak v_all v_scaled "
                         "stat ln dve rows_out veps")
        ids, fs = early["ids"], [fq, fo, early["wkv"], early["ctx"]]
        mat_in = [s.sem("wq_in"), s.sem("wo_in")] + early["loaded"][0:2]
        x_loaded = [s.sem(f"x_loaded{i}") for i in range(XB)]
        pairs = [keep["wq"], keep["wo"], kv_w, cx]

        def flat(t):
            return t.rearrange("p a b c -> p (a b c)") if len(t.shape) == 4 else t.rearrange("p a b -> p (a b)")

        with nc.Block() as block:
            @block.sync
            def _(sp):
                sp.dma_start(fq[:, :], wq_t).then_inc(mat_in[0], 16)
                sp.dma_start(fo[:, :], wo_t).then_inc(mat_in[1], 16)
                sp.wait_ge(m["split_lo"], 2)
                for g in range(NT // XG):
                    need(sp, m["stat"], (g - XB + 1) * XG)
                    sp.dma_start(xg[:, g % XB], x[g * XG * P:(g + 1) * XG * P, :].rearrange(
                        "(n p) d -> p n d", p=P)).then_inc(x_loaded[g % XB], 16)

            @block.vector
            def _(dve):
                link = chain(dve, m["dve"])
                for i in (3, 2, 0, 1):
                    dve.wait_ge(mat_in[i], 16)
                    last = nc.vector.tensor_reduce(peaks[:, i:i + 1], fs[i][:, :], AX.X, ALU.max, apply_absolute_value=True)
                last.then_inc(m["peaks"], 1)
                link(nc.vector.memset(vcol[:, :], 0.0))
                dve.wait_ge(early["loaded"][2], 16)
                link(nc.vector.tensor_scalar(idf[:, :], ids[:, :], 0.0, float(LKV + 2), ALU.max, ALU.min))
                for j in range(W):
                    nc.vector.tensor_scalar(keep["mask"][:, :, j], idf[:, :], float(3 - j), LOW, ALU.is_lt, ALU.mult)
                for b in range(B):
                    link(nc.vector.tensor_scalar(keep["rows"][:, b * PER:(b + 1) * PER], idf[:, b * PER:(b + 1) * PER],
                                                 float(b * ROWS), None, ALU.add))
                dve.wait_ge(m["all"], 1)
                link(nc.vector.tensor_scalar(keep["alpha"][:, 0:4], allp[:, :], 1e-30, 1.0 / SPAN, ALU.max, ALU.mult))
                nc.vector.reciprocal(unit[:, :], keep["alpha"][:, 0:4]).then_inc(m["unit"], 1)
                dve.wait_ge(m["unit"], 1)
                for n, i in enumerate((3, 2, 0, 1)):
                    (hi, lo), f = pairs[i], fs[i]
                    link(nc.vector.tensor_scalar(f[:, :], f[:, :], unit[:, i:i + 1], None, ALU.mult))
                    link(nc.vector.tensor_copy(flat(hi[:]), f[:, :]))
                    nc.vector.tensor_tensor(flat(lo[:]), f[:, :], flat(hi[:]), ALU.subtract).then_inc(m["split_lo"], 1)
                for t in range(NT):
                    if t % XG == 0:
                        dve.wait_ge(x_loaded[t // XG % XB], 16 * (t // XG // XB + 1))
                    nc.vector.bn_stats(stats[:, t, :], xg[:, t // XG % XB, t % XG, :]).then_inc(m["stat"], 1)
                    if t == NT * 5 // 8:
                        dve.wait_ge(m["v_out"], 2 * B)
                        for i in range(2 * B):
                            rows = P if i % 2 == 0 else TAIL
                            last = nc.vector.tensor_reduce(vcol[0:rows, i:i + 1], kv[0:rows, i, D:2 * D], AX.X, ALU.max,
                                                           apply_absolute_value=True)
                        link(last)
                        nc.vector.tensor_reduce(vred[:, :], vcol[:, :], AX.X, ALU.max).then_inc(m["v_peak"], 1)
                    if t == NT * 3 // 4:
                        dve.wait_ge(m["v_all"], 1)
                        link(nc.vector.tensor_scalar(vinv[:, :], vall[:, :], 1e-30, 1.0 / VSPAN, ALU.max, ALU.mult))
                        nc.vector.tensor_copy(keep["alpha"][:, 7:8], vinv[:, :])
                        link(nc.vector.reciprocal(unit[:, 0:1], vinv[:, :]))
                        dve.wait_ge(m["k_out"], 2 * B)
                        for i in range(2 * B):
                            rows = P if i % 2 == 0 else TAIL
                            last = nc.vector.tensor_scalar(kv[0:rows, i, D:2 * D], kv[0:rows, i, D:2 * D], unit[0:rows, 0:1], None, ALU.mult)
                        last.then_inc(m["v_scaled"], 1)
                dve.wait_ge(m["stat"], NT)
                for t in range(NT):
                    last = nc.vector.bn_aggr(mv[:, t, :], stats[:, t, :])
                link(last)
                nc.vector.tensor_scalar(veps[:, :], mv[:, :, 1], EPS, None, ALU.add).then_inc(m["veps"], 1)
                dve.wait_ge(m["ln"], 2)
                link(nc.vector.tensor_tensor(y1[:, :], y0[:, :], y0[:, :], ALU.mult))
                link(nc.vector.tensor_tensor(y2[:, :], y1[:, :], veps[:, :], ALU.mult))
                link(nc.vector.tensor_scalar(y1[:, :], y2[:, :], -0.5, 1.5, ALU.mult, ALU.add))
                link(nc.vector.tensor_tensor(keep["rstd"][:, :], y0[:, :], y1[:, :], ALU.mult))
                link(nc.vector.scalar_tensor_tensor(out=keep["shift"][:, :], in0=mv[:, :, 0], scalar=-1.0,
                                                    in1=keep["rstd"][:, :], op0=ALU.mult, op1=ALU.mult))
                al = keep["alpha"]
                link(nc.vector.tensor_tensor(al[:, 8:9], al[:, 2:3], al[:, 3:4], ALU.mult))
                link(nc.vector.tensor_scalar(al[:, 9:10], al[:, 8:9], al[:, 0:1], float(HD) ** -0.5, ALU.mult, ALU.mult))
                link(nc.vector.tensor_scalar(al[:, 10:11], al[:, 8:9], al[:, 1:2], al[:, 7:8], ALU.mult, ALU.mult))

            @block.scalar
            def _(act):
                for i in range(2 * B):
                    rows = P if i % 2 == 0 else TAIL
                    for half in range(2):
                        n = 2 * i + half
                        act.wait_ge(m["kv_ready"], n + 1)
                        nc.scalar.activation(kv[0:rows, i, half * D:(half + 1) * D], pk[n % 8][0:rows, :],
                                             ACT.Copy).then_inc(m["v_out" if half else "k_out"], 1)
                act.wait_ge(m["v_scaled"], 1)
                for b in range(B):
                    lo, hi = kv[:, 2 * b, :], kv[:, 2 * b + 1, :]
                    act.dma_start(table[b * ROWS + 3:b * ROWS + 3 + P, :], lo).then_inc(m["rows_out"], 16)
                    act.dma_start(table[b * ROWS + 3 + P:b * ROWS + 3 + LKV, :], hi[0:TAIL]).then_inc(m["rows_out"], 16)
                    for j in range(3):
                        act.dma_start(table[b * ROWS + j:b * ROWS + j + 1, :], lo[0:1]).then_inc(m["rows_out"], 16)
                        act.dma_start(table[b * ROWS + 3 + LKV + j:b * ROWS + 4 + LKV + j, :],
                                     hi[TAIL - 1:TAIL]).then_inc(m["rows_out"], 16)
                act.wait_ge(m["veps"], 1)
                nc.scalar.activation(lnv[:, :], veps[:, :], ACT.Ln).then_inc(m["ln"], 1)
                act.wait_ge(m["ln"], 1)
                nc.scalar.activation(y0[:, :], lnv[:, :], ACT.Exp, scale=-0.5).then_inc(m["ln"], 1)
                act.wait_ge(m["rows_out"], 16 * 8 * B)

            @block.gpsimd
            def _(pool):
                pool.wait_ge(m["peaks"], 1)
                nc.gpsimd.partition_all_reduce(allp[:, :], peaks[:, :], P, PEAK).then_inc(m["all"], 1)
                pool.wait_ge(m["v_peak"], 1)
                nc.gpsimd.partition_all_reduce(vall[:, :], vred[:, :], P, PEAK).then_inc(m["v_all"], 1)

            @block.tensor
            def _(pe):
                pe.wait_ge(m["split_lo"], 2)
                for i in range(2 * B):
                    b, r0, rows = i // 2, (0, P)[i % 2], (P, TAIL)[i % 2]
                    for half in range(2):
                        n = 2 * i + half
                        if n >= 8:
                            pe.wait_ge(m["v_out" if half else "k_out"], (n - 8) // 2 + 1)
                        todo = [(a, w, c) for c in range(DC) for a, w in ((0, 0), (0, 1), (1, 0))]
                        for q, (a, w, c) in enumerate(todo):
                            mm = nc.tensor.matmul(pk[n % 8][0:rows, :], cx[a][:, c, b, r0:r0 + rows],
                                                  kv_w[w][:, c, half * D:(half + 1) * D],
                                                  start=(q == 0), stop=(q == len(todo) - 1))
                        mm.then_inc(m["kv_ready"], 1)


def prepare_quant(nc, keep, early, gate_n, up_n, down_n):
    NB = FC * D // QB
    with Scope(nc, "pq") as s:
        nat = s.sb("nat", [P, 2, FC * D], F32)
        q16 = s.sb("q16", [P, FC * D], I16)
        nhi, nlo = (s.sb(n, [P, FC * D], F16) for n in ("nhi", "nlo"))
        peak, sc, rs, su = (s.sb(n, [P, NB], F32) for n in ("peak", "sc", "rs", "su"))
        red, allm, unit = (s.sb(n, [P, 1], F32) for n in ("red", "allm", "unit_w"))
        pt = [s.ps(f"pt{i}", [P, 4 * P], F16) for i in range(4)]
        loaded = [s.sem(f"loaded{i}") for i in range(3)]
        half_in = s.sem("half_in")
        m = s.sems("red all dve scaled hi lo turned out")
        mats = [(gate_n, keep["gate"], 4), (up_n, keep["up"], 5), (down_n, keep["down"], 6)]

        with nc.Block() as block:
            @block.sync
            def _(sp):
                half = FC * D // 2
                sp.dma_start(nat[:, 0, 0:half], mats[0][0][:, 0:half]).then_inc(half_in, 16)
                sp.dma_start(nat[:, 0, half:], mats[0][0][:, half:]).then_inc(loaded[0], 16)
                sp.dma_start(nat[:, 1, :], mats[1][0]).then_inc(loaded[1], 16)
                for i, (dst, src) in enumerate(early["loads"]):
                    sp.dma_start(dst[:, :], src).then_inc(early["loaded"][i], 16)
                sp.wait_ge(m["lo"], 1)
                sp.dma_start(nat[:, 0, :], mats[2][0]).then_inc(loaded[2], 16)

            @block.vector
            def _(dve):
                link = chain(dve, m["dve"])

                def wide(t):
                    return t[:, :].unsqueeze(2).to_broadcast([P, NB, QB])

                def blocks(i):
                    return nat[:, i % 2, :].rearrange("p (n k) -> p n k", k=QB)

                def find_peaks(i):
                    dve.wait_ge(loaded[i], 16)
                    link(nc.vector.tensor_reduce(peak[:, :], blocks(i), AX.X, ALU.max, apply_absolute_value=True))

                def split(i, sem):
                    dve.wait_ge(m["hi"], i + 1)
                    need(dve, m["turned"], 12 * i * 2)
                    nc.vector.tensor_tensor(nlo[:, :], nat[:, i % 2, :], nhi[:, :], ALU.subtract).then_inc(sem, 1)

                dve.wait_ge(half_in, 16)
                nc.vector.tensor_reduce(peak[:, 0:NB // 2], blocks(0)[:, 0:NB // 2], AX.X, ALU.max, apply_absolute_value=True)
                dve.wait_ge(loaded[0], 16)
                link(nc.vector.tensor_reduce(peak[:, NB // 2:], blocks(0)[:, NB // 2:], AX.X, ALU.max, apply_absolute_value=True))
                for i, (_, _, a) in enumerate(mats):
                    w, q = blocks(i), q16[:, :].rearrange("p (n k) -> p n k", k=QB)
                    link(nc.vector.tensor_scalar(sc[:, :], peak[:, :], 1.0 / WMAX, TINY, ALU.mult, ALU.max))
                    link(nc.vector.reciprocal(rs[:, :], sc[:, :]))
                    nc.vector.tensor_reduce(red[:, :], sc[:, :], AX.X, ALU.max).then_inc(m["red"], 1)
                    need(dve, m["scaled"], i)
                    link(nc.vector.tensor_tensor(q, w, wide(rs), ALU.mult))
                    if i == 0:
                        find_peaks(1)
                    if i == 1:
                        split(0, m["lo"])
                    dve.wait_ge(m["all"], i + 1)
                    link(nc.vector.tensor_scalar(keep["alpha"][:, a:a + 1], allm[:, :], WMAX / SPAN, None, ALU.mult))
                    link(nc.vector.reciprocal(unit[:, :], keep["alpha"][:, a:a + 1]))
                    link(nc.vector.tensor_scalar(su[:, :], sc[:, :], unit[:, 0:1], None, ALU.mult))
                    nc.vector.tensor_tensor(w, q, wide(su), ALU.mult).then_inc(m["scaled"], 1)
                    if i == 1:
                        find_peaks(2)
                dve.wait_ge(m["lo"], 2)
                split(2, m["lo"])

            @block.scalar
            def _(act):
                for i, (_, dst, _) in enumerate(mats):
                    act.wait_ge(m["scaled"], i + 1)
                    need(act, m["turned"], 12 * i * 2)
                    nc.scalar.activation(nhi[:, :], nat[:, i % 2, :], ACT.Copy).then_inc(m["hi"], 1)
                    for g in range(24):
                        part, r = g // 12, g % 12
                        act.wait_ge(m["turned"], 24 * i + g + 1)
                        out = dst[part][:, :, r * P:(r + 1) * P] if i < 2 else dst[part][:, r, :]
                        src = pt[g % 4][:, :].rearrange("p (c n) -> p c n", c=4) if i < 2 else pt[g % 4][:, :]
                        nc.scalar.activation(out, src, ACT.Copy).then_inc(m["out"], 1)

            @block.gpsimd
            def _(pool):
                for i in range(3):
                    pool.wait_ge(m["red"], i + 1)
                    need(pool, m["scaled"], i)
                    nc.gpsimd.partition_all_reduce(allm[:, :], red[:, :], P, PEAK).then_inc(m["all"], 1)
                    if i == 1:
                        pool.wait_ge(m["hi"], 2)
                        pool.wait_ge(m["turned"], 24)
                        nc.gpsimd.tensor_tensor(nlo[:, :], nat[:, 1, :], nhi[:, :], ALU.subtract).then_inc(m["lo"], 1)

            @block.tensor
            def _(pe):
                for i in range(3):
                    for g in range(24):
                        part, r = g // 12, g % 12
                        if r == 0:
                            pe.wait_ge(m["lo" if part else "hi"], i + 1)
                        need(pe, m["out"], 24 * i + g - 3)
                        src = (nlo if part else nhi)[:, :]
                        for c in range(4):
                            at = r * D + c * P if i < 2 else c * F + r * P
                            mm = nc.tensor.transpose(pt[g % 4][:, c * P:(c + 1) * P], src[:, at:at + P], keep["ident16"][:, :])
                        mm.then_inc(m["turned"], 1)


def attention(nc, keep, x, table, x1_d, hT_d, B):
    T = x.shape[0]
    NT = T // P
    U = 8
    KR = 4
    with Scope(nc, "at") as s:
        xs = s.sb("xs", [P, U, D], F32)
        kv = s.sb("kv_rows", [P, KR, W, 2 * D], F32)
        xn, att, hn = (s.sb(n, [P, 2, D], F32) for n in ("xn", "att", "hn"))
        xhi, xlo, ahi, alo = (s.sb(n, [P, 2, DC, P], F16) for n in ("xhi", "xlo", "ahi", "alo"))
        hT = s.sb("hT", [P, 4, D], F32)
        raw, sc, ds, ex, pr = (s.sb(n, [P, W, H], F32) for n in ("raw", "sc", "ds", "ex", "pr"))
        top, tot, inv = (s.sb(n, [P, H], F32) for n in ("top", "tot", "inv"))
        passed = s.sb("passed", [P, D], F32)
        nmean, ssq, rstd, shift = (s.sb(n, [P, 2], F32) for n in ("nmean", "ssq", "rstd2", "shift2"))
        sqe, root = s.sb("sqe", [P, 1], F32), s.sb("root", [P, 1], F32)
        eps_d, expo, root_d = (s.sb(n, [P, 1], F32) for n in ("eps_d", "expo", "root_d"))
        psX, psA = s.ps("psX", [P, DC, P]), s.ps("psA", [P, DC, P])
        psQ = [s.ps(f"psQ{i}", [P, D]) for i in range(2)]
        psO = [s.ps(f"psO{i}", [P, D]) for i in range(2)]
        psH = [s.ps(f"psH{i}", [P, DC, P]) for i in range(2)]
        x_in, x1_out, hT_out = Transfers(s, "x_in", U), Transfers(s, "x1_out", U), Transfers(s, "hT_out", 4)
        rows_in = Transfers(s, "rows_in", KR, 16 * W)
        m = s.sems("xn xT xhi xrest xlo arest q prod raw sc top ds ex tot inv pr pv half att aT ahi alo o x1 "
                         "nmean ssq sqe root rstd norm hn hT hT_sb peak consts")
        wq, wo, ident = keep["wq"], keep["wo"], keep["ident32"]
        x_v = x.rearrange("(n p) d -> p n d", p=P)

        with nc.Block() as block:
            @block.sync
            def _(sp):
                def tick(c):
                    at, live, u = c.at, c.live, c.u
                    if live(4):
                        if u == 0:
                            x1_out.done(sp, c, -4)
                            need(sp, m["hn"], at(-3))
                        else:
                            need(sp, m["hn"], at(-3))
                            x1_out.done(sp, c, -4)
                        sp.dma_start(xs[:, (u + 4) % U, :], x_v[:, bass.ds(at(4), 1), :]).then_inc(x_in.of(c, 4), 16)
                    if live(-2):
                        need(sp, m["x1"], at(-1))
                        sp.dma_start(x1_d[bass.ds(at(-2), 1), :, :].rearrange("a p d -> p (a d)"), xs[:, (u - 2) % U, :]).then_inc(x1_out.of(c, -2), 16)
                    if live(-4):
                        need(sp, m["hT_sb"], at(-3))
                        sp.dma_start(hT_d[bass.ds(at(-4), 1)].rearrange("a p d -> p (a d)"), hT[:, (u - 4) % 4, :]).then_inc(hT_out.of(c, -4), 16)
                pipeline(sp, tick, NT, U, before=4, after=4)
                x1_out.all_done(sp, NT)
                hT_out.all_done(sp, NT)

            @block.scalar
            def _(act):
                def tick(c):
                    at, live, u = c.at, c.live, c.u
                    if live(2):
                        need(act, m["xT"], at(3))
                        need(act, m["q"], at(1))
                        nc.scalar.activation(xhi[:, u % 2], psX[:, :, :], ACT.Copy).then_inc(m["xhi"], 1)
                    if live(-3):
                        need(act, m["norm"], at(-2))
                        need(act, m["hT"], at(-4))
                        k = (u - 3) % 2
                        nc.scalar.activation(hn[:, k, :], xs[:, (u - 3) % U, :], ACT.Identity,
                                             bias=shift[:, k:k + 1], scale=rstd[:, k:k + 1]).then_inc(m["hn"], 1)
                    if live(-2):
                        need(act, m["x1"], at(-1))
                        nc.scalar.activation(passed[:, :], xs[:, (u - 2) % U, :], ACT.Identity, scale=-1.0 / D,
                                             accum_out=nmean[:, u % 2:u % 2 + 1]).then_inc(m["nmean"], 1)
                    if live(-1):
                        need(act, m["aT"], at(0))
                        need(act, m["o"], at(-2))
                        nc.scalar.activation(ahi[:, (u - 1) % 2], psA[:, :, :], ACT.Copy).then_inc(m["ahi"], 1)
                    if live(0):
                        need(act, m["ds"], at(1))
                        need(act, m["pr"], at(0))
                        nc.scalar.activation(ex[:, :, :], ds[:, :, :], ACT.Exp).then_inc(m["ex"], 1)
                    if live(2):
                        need(act, m["xrest"], at(3))
                        nc.scalar.activation(xlo[:, u % 2], psX[:, :, :], ACT.Copy).then_inc(m["xlo"], 1)
                    if live(-2):
                        need(act, m["nmean"], at(-1))
                        nc.scalar.activation(passed[:, :], xs[:, (u - 2) % U, :], ACT.Square, bias=nmean[:, u % 2:u % 2 + 1],
                                             accum_out=ssq[:, u % 2:u % 2 + 1]).then_inc(m["ssq"], 1)
                    if live(-1):
                        need(act, m["arest"], at(0))
                        nc.scalar.activation(alo[:, (u - 1) % 2], psA[:, :, :], ACT.Copy).then_inc(m["alo"], 1)
                    if live(3):
                        x_in.done(act, c, 3)
                        need(act, m["xrest"], at(2))
                        nc.scalar.activation(xn[:, (u + 3) % 2, :], xs[:, (u + 3) % U, :], ACT.Identity,
                                             bias=keep["shift"][:, bass.ds(at(3), 1)],
                                             scale=keep["rstd"][:, bass.ds(at(3), 1)]).then_inc(m["xn"], 1)
                    if live(-3):
                        need(act, m["hT"], at(-2))
                        hT_out.done(act, c, -7)
                        need(act, m["peak"], at(-6))
                        nc.scalar.activation(hT[:, (u - 3) % 4, :], psH[(u - 3) % 2][:, :, :].rearrange("p c t -> p (c t)"),
                                             ACT.Copy).then_inc(m["hT_sb"], 1)
                pipeline(act, tick, NT, U, before=3, after=3)

            @block.vector
            def _(dve):
                nc.vector.memset(eps_d[:, :], EPS * D)
                nc.vector.memset(expo[:, :], -0.5)
                nc.vector.memset(root_d[:, :], float(D) ** 0.5).then_inc(m["consts"], 1)

                def tick(c):
                    at, live, u = c.at, c.live, c.u
                    if live(0):
                        keys = kv[:, u % KR, :, 0:D]
                        rows_in.done(dve, c)
                        need(dve, m["q"], at(1))
                        nc.vector.tensor_tensor(keys, keys, psQ[u % 2][:, :].unsqueeze(1).to_broadcast([P, W, D]),
                                                ALU.mult).then_inc(m["prod"], 1)
                    if live(-2):
                        need(dve, m["o"], at(-1))
                        nc.vector.scalar_tensor_tensor(out=xs[:, (u - 2) % U, :], in0=psO[(u - 2) % 2][:, :],
                                                       scalar=keep["alpha"][:, 10:11], in1=xs[:, (u - 2) % U, :],
                                                       op0=ALU.mult, op1=ALU.add).then_inc(m["x1"], 1)
                    if live(0):
                        need(dve, m["prod"], at(1))
                        nc.vector.tensor_reduce(raw[:, :, :], keys.rearrange("p w (h e) -> p w h e", h=H),
                                                AX.X, ALU.add).then_inc(m["raw"], 1)
                    if live(0):
                        need(dve, m["raw"], at(1))
                        nc.vector.scalar_tensor_tensor(
                            out=sc[:, :, :], in0=raw[:, :, :], scalar=keep["alpha"][:, 9:10],
                            in1=keep["mask"][:, bass.ds(at(0), 1), :].rearrange("p a w -> p (a w)").unsqueeze(2).to_broadcast([P, W, H]),
                            op0=ALU.mult, op1=ALU.add).then_inc(m["sc"], 1)
                    if live(0):
                        need(dve, m["sc"], at(1))
                        nc.vector.tensor_reduce(top[:, :], sc[:, :, :].rearrange("p w h -> p h w"), AX.X,
                                                ALU.max).then_inc(m["top"], 1)
                    if live(0):
                        need(dve, m["top"], at(1))
                        nc.vector.tensor_tensor(ds[:, :, :], sc[:, :, :], top[:, :].unsqueeze(1).to_broadcast([P, W, H]),
                                                ALU.subtract).then_inc(m["ds"], 1)
                    if live(-4):
                        need(dve, m["hT_sb"], at(-3))
                        nc.vector.tensor_reduce(keep["h_peak"][:, bass.ds(at(-4), 1)], hT[:, (u - 4) % 4, :],
                                                AX.X, ALU.max, apply_absolute_value=True).then_inc(m["peak"], 1)
                    if live(0):
                        need(dve, m["ex"], at(1))
                        nc.vector.tensor_reduce(tot[:, :], ex[:, :, :].rearrange("p w h -> p h w"), AX.X,
                                                ALU.add).then_inc(m["tot"], 1)
                        need(dve, m["tot"], at(1))
                        nc.vector.reciprocal(inv[:, :], tot[:, :]).then_inc(m["inv"], 1)
                        need(dve, m["inv"], at(1))
                        nc.vector.tensor_tensor(pr[:, :, :], ex[:, :, :], inv[:, :].unsqueeze(1).to_broadcast([P, W, H]),
                                                ALU.mult).then_inc(m["pr"], 1)
                        need(dve, m["pr"], at(1))
                        values = kv[:, u % KR, :, D:2 * D].rearrange("p w (h e) -> p w h e", h=H)
                        nc.vector.tensor_tensor(values, values, pr[:, :, :].unsqueeze(3).to_broadcast([P, W, H, HD]),
                                                ALU.mult).then_inc(m["pv"], 1)
                pipeline(dve, tick, NT, U, after=4)

            @block.gpsimd
            def _(pool):
                def gather(t):
                    if t < NT:
                        for j in range(W):
                            pool.indirect_dma_start(out=kv[:, t % KR, j, :], out_offset=None, in_=table,
                                                    in_offset=bass.IndirectOffsetOnAxis(ap=keep["rows"][:, t:t + 1], axis=0),
                                                    element_offset=j * 2 * D).then_inc(rows_in.sems[t % KR], 16)

                def norm(t):
                    if t < 0:
                        return
                    k = slice(t % 2, t % 2 + 1)
                    pool.wait_ge(m["ssq"], t + 1)
                    nc.gpsimd.tensor_tensor(sqe[:, :], ssq[:, k], eps_d[:, :], ALU.add).then_inc(m["sqe"], 1)
                    pool.wait_ge(m["sqe"], t + 1)
                    nc.gpsimd.tensor_tensor(root[:, :], sqe[:, :], expo[:, :], ALU.pow).then_inc(m["root"], 1)
                    pool.wait_ge(m["root"], t + 1)
                    need(pool, m["hn"], t - 1)
                    nc.gpsimd.tensor_tensor(rstd[:, k], root[:, :], root_d[:, :], ALU.mult).then_inc(m["rstd"], 1)
                    pool.wait_ge(m["rstd"], t + 1)
                    nc.gpsimd.tensor_tensor(shift[:, k], nmean[:, k], rstd[:, k], ALU.mult).then_inc(m["norm"], 1)

                pool.wait_ge(m["consts"], 1)
                for t in range(KR):
                    gather(t)
                for t in range(NT):
                    lower, upper = kv[:, t % KR, 0:2, D:2 * D], kv[:, t % KR, 2:4, D:2 * D]
                    pool.wait_ge(m["pv"], t + 1)
                    nc.gpsimd.tensor_tensor(lower, lower, upper, ALU.add).then_inc(m["half"], 1)
                    pool.wait_ge(m["half"], t + 1)
                    need(pool, m["arest"], t - 1)
                    nc.gpsimd.tensor_tensor(att[:, t % 2, :], kv[:, t % KR, 0, D:2 * D], kv[:, t % KR, 1, D:2 * D],
                                            ALU.add).then_inc(m["att"], 1)
                    pool.wait_ge(m["att"], t + 1)
                    gather(t + KR)
                    norm(t - 1)
                norm(NT - 1)

            @block.tensor
            def _(pe):
                def project(out, hi, lo, w, slot):
                    todo = [(a, b, c) for c in range(DC) for a, b in ((hi, 0), (hi, 1), (lo, 0))]
                    for q, (a, b, c) in enumerate(todo):
                        mm = nc.tensor.matmul(out[:, :], a[:, slot, c, :], w[b][:, c, :],
                                              start=(q == 0), stop=(q == len(todo) - 1))
                    return mm

                def turn(out, a):
                    for c in range(DC):
                        mm = nc.tensor.transpose(out[:, c, :], a[:, c * P:(c + 1) * P], ident[:, :])
                    return mm

                def turn_rest(out, a, hi):
                    nc.tensor.matmul(out[:, :, :].rearrange("p c t -> p (c t)"), keep["neg16"][:, :],
                                     hi.rearrange("p c t -> p (c t)"), start=True, stop=False)
                    for c in range(DC):
                        mm = nc.tensor.matmul(out[:, c, :], a[:, c * P:(c + 1) * P], ident[:, :], start=False, stop=(c == DC - 1))
                    return mm

                def tick(c):
                    at, live, u = c.at, c.live, c.u
                    if live(2):
                        need(pe, m["xn"], at(3))
                        need(pe, m["xlo"], at(2))
                        turn(psX, xn[:, u % 2, :]).then_inc(m["xT"], 1)
                    if live(1):
                        need(pe, m["xlo"], at(2))
                        need(pe, m["prod"], at(0))
                        project(psQ[(u + 1) % 2], xhi, xlo, wq, (u + 1) % 2).then_inc(m["q"], 1)
                    if live(2):
                        need(pe, m["xhi"], at(3))
                        turn_rest(psX, xn[:, u % 2, :], xhi[:, u % 2]).then_inc(m["xrest"], 1)
                    if live(-1):
                        need(pe, m["att"], at(0))
                        need(pe, m["alo"], at(-1))
                        turn(psA, att[:, (u - 1) % 2, :]).then_inc(m["aT"], 1)
                    if live(-3):
                        need(pe, m["hn"], at(-2))
                        need(pe, m["hT_sb"], at(-4))
                        turn(psH[(u - 3) % 2], hn[:, (u - 3) % 2, :]).then_inc(m["hT"], 1)
                    if live(-1):
                        need(pe, m["ahi"], at(0))
                        turn_rest(psA, att[:, (u - 1) % 2, :], ahi[:, (u - 1) % 2]).then_inc(m["arest"], 1)
                        need(pe, m["alo"], at(0))
                        need(pe, m["x1"], at(-2))
                        project(psO[(u - 1) % 2], ahi, alo, wo, (u - 1) % 2).then_inc(m["o"], 1)
                pipeline(pe, tick, NT, U, before=2, after=3)


def whole_peak(nc, s, m, name, cols):
    red, out = s.sb(f"{name}_red", [P, 1], F32), s.sb(f"{name}_all", [P, 1], F32)

    def on_vector(dve):
        nc.vector.tensor_reduce(red[:, :], cols, AX.X, ALU.max).then_inc(m[f"{name}_red"], 1)

    def on_pool(pool):
        pool.wait_ge(m[f"{name}_red"], 1)
        nc.gpsimd.partition_all_reduce(out[:, :], red[:, :], P, PEAK).then_inc(m[f"{name}_all"], 1)
    return out, on_vector, on_pool


def quantiser(nc, link, scale, inv, peak, unit):
    link(nc.vector.tensor_scalar(scale, peak, unit, 1.0 / QMAX, ALU.mult, ALU.mult))
    link(nc.vector.tensor_scalar(scale, scale, TINY, None, ALU.max))
    link(nc.vector.reciprocal(inv, scale))
    link(nc.vector.tensor_tensor(inv, inv, unit, ALU.mult))


def feed_in(nc, keep, hT_d, raw_d, NB, gate_d=None, gate_q=None):
    up = gate_d is not None
    name = "up" if up else "ga"
    wt = keep["up" if up else "gate"]
    g = keep["g"]
    U = 2
    PAIRS = FC // 2
    with Scope(nc, name) as s:
        hT_v = hT_d.rearrange("(b n) p d -> b p n d", n=SUB)
        hb = s.sb("hb", [P, 2, SUB, D], F32)
        hq = s.sb("hq", [P, DC * BLK], I16)
        ah, al = (s.sb(n, [P, 2, SUB, DC, P], F16) for n in ("ah", "al"))
        raw = s.sb("raw", [P, 3, UE], F32)
        pp = [s.ps(f"pp{i}", [P, 2, BLK]) for i in range(4)]
        h_in, stored = Transfers(s, "h_in", 2), Transfers(s, "stored", UNITS)
        gate_in, gate_out = Transfers(s, "gate_in", 3), Transfers(s, "gate_out", 2)
        m = s.sems("h_red h_all g_red g_all dve scales hq ah al mm out peak gq sig sq prod gpeak")
        if up:
            gin, gp = s.sb("gin", [P, 3, UE], F32), s.sb("gp", [P, 2, UE], F32)
            sig = s.sb("sig", [P, 2, UE], F32)
            gq, sq = s.sb("gq", [P, 2, UE], I16), s.sb("sq", [P, 2, UE], U16)
            gate_u = gate_d.rearrange("b q p d -> (b q) p d")
            peak, peak_v, peak_p = whole_peak(nc, s, m, "g", keep["gate_peak"][:, :])
        else:
            peak, peak_v, peak_p = whole_peak(nc, s, m, "h", keep["h_peak"][:, :])
        out_peak = keep["up_peak" if up else "gate_peak"]

        with nc.Block() as block:
            @block.sync
            def _(sp):
                def tick(c):
                    at, live, u = c.at, c.live, c.u
                    if live(2):
                        need(sp, m["hq"], at(1))
                        sp.dma_start(hb[:, u % 2], hT_v[bass.ds(at(2), 1)].rearrange("a p n d -> p (a n) d")).then_inc(h_in.of(c, 2), 16)
                    for q in range(UNITS):
                        n = at(0) * UNITS + q
                        if up and c.live_unit(UNITS, q + 3):
                            need(sp, m["gq"], n + 1)
                            sp.dma_start(gin[:, q, :], gate_u[bass.ds(n + 3, 1)].rearrange("a p d -> p (a d)")).then_inc(gate_in.of(c, 0, UNITS, q + 3), 16)
                        if up and c.live_unit(UNITS, q + 1):
                            need(sp, m["gq"], n + 2)
                            sp.dma_start(gate_q[bass.ds(n + 1, 1)].rearrange("a p d -> p (a d)"),
                                         gq[:, (u * UNITS + q + 1) % 2, :]).then_inc(gate_out.of(c, 0, UNITS, q + 1), 16)
                        if live(0):
                            need(sp, m["peak"], n + 1)
                            sp.dma_start(raw_d[bass.ds(at(0), 1), q].rearrange("a p d -> p (a d)"), raw[:, q, :]).then_inc(stored.of(c, 0, UNITS, q), 16)
                pipeline(sp, tick, NB, U, before=2)
                stored.all_done(sp, UNITS * NB)
                if up:
                    gate_out.all_done(sp, UNITS * NB)

            @block.gpsimd
            def _(pool):
                peak_p(pool)

            @block.vector
            def _(dve):
                link = chain(dve, m["dve"])
                peak_v(dve)
                if not up:
                    dve.wait_ge(m["h_all"], 1)
                    link(nc.vector.memset(g[:, 15:16], 1.0))
                    quantiser(nc, link, g[:, 0:1], g[:, 1:2], peak[:, :], g[:, 15:16])
                    link(nc.vector.tensor_tensor(g[:, 2:3], g[:, 0:1], keep["alpha"][:, 4:5], ALU.mult))
                    link(nc.vector.tensor_tensor(g[:, 3:4], g[:, 0:1], keep["alpha"][:, 5:6], ALU.mult))
                else:
                    dve.wait_ge(m["g_all"], 1)
                    quantiser(nc, link, g[:, 4:5], g[:, 5:6], peak[:, :], g[:, 2:3])
                nc.vector.memset(g[:, 14:15], 0.0).then_inc(m["scales"], 1)

                def tick(c):
                    at, live, u = c.at, c.live, c.u
                    if live(1):
                        a = (u + 1) % 2
                        need(dve, m["hq"], at(2))
                        need(dve, m["mm"], at(0) * PAIRS)
                        nc.vector.tensor_copy(ah[:, a].rearrange("p n c t -> p (n c t)"), hq[:, :]).then_inc(m["ah"], 1)
                        need(dve, m["ah"], at(2))
                        nc.vector.tensor_tensor(al[:, a].rearrange("p n c t -> p (n c t)"), hq[:, :],
                                                ah[:, a].rearrange("p n c t -> p (n c t)"), ALU.subtract).then_inc(m["al"], 1)
                    for q in range(UNITS):
                        n = at(0) * UNITS + q
                        if up and c.live_unit(UNITS, q + 1):
                            k = (u * UNITS + q + 1) % 2
                            need(dve, m["sig"], n + 2)
                            need(dve, m["prod"], n)
                            nc.vector.tensor_scalar(sq[:, k, :], sig[:, k, :], 65536.0, 65535.0, ALU.mult, ALU.min).then_inc(m["sq"], 1)
                            need(dve, m["sq"], n + 2)
                            need(dve, m["gpeak"], n)
                            nc.vector.tensor_tensor(gp[:, k, :], gq[:, k, :], sq[:, k, :], ALU.mult).then_inc(m["prod"], 1)
                            need(dve, m["prod"], n + 2)
                            nc.vector.tensor_reduce(keep["gated_peak"][:, bass.ds(n + 1, 1)], gp[:, k, :], AX.X, ALU.max,
                                                    apply_absolute_value=True).then_inc(m["gpeak"], 1)
                        if live(0):
                            need(dve, m["out"], n * 2 + 2)
                            nc.vector.tensor_reduce(out_peak[:, bass.ds(n, 1)], raw[:, q, :], AX.X, ALU.max,
                                                    apply_absolute_value=True).then_inc(m["peak"], 1)
                pipeline(dve, tick, NB, U, before=1)

            @block.scalar
            def _(act):
                if not up:
                    act.wait_ge(m["scales"], 1)

                def tick(c):
                    at, live, u = c.at, c.live, c.u
                    def quantise_next():
                        if live(1):
                            h_in.done(act, c, 1)
                            need(act, m["al"], at(1))
                            nc.scalar.activation(hq[:, :], hb[:, (u + 1) % 2].rearrange("p n d -> p (n d)"), ACT.Copy, scale=g[:, 1:2]).then_inc(m["hq"], 1)
                    if not live(0):
                        quantise_next()
                    for q in range(UNITS):
                        n = at(0) * UNITS + q
                        if up and c.live_unit(UNITS, q + 1):
                            k = (u * UNITS + q + 1) % 2
                            if c.first(0, UNITS, q + 1):
                                act.wait_ge(m["scales"], 1)
                            gate_in.done(act, c, 0, UNITS, q + 1)
                            need(act, m["prod"], n)
                            gate_out.done(act, c, 0, UNITS, q - 1)
                            nc.scalar.activation(gq[:, k, :], gin[:, (q + 1) % 3, :], ACT.Copy, scale=g[:, 5:6]).then_inc(m["gq"], 1)
                            need(act, m["gq"], n + 2)
                            need(act, m["sq"], n)
                            nc.scalar.activation(sig[:, k, :], gq[:, k, :], ACT.Sigmoid, scale=g[:, 4:5]).then_inc(m["sig"], 1)
                        if not live(0):
                            continue
                        for h in range(2):
                            pair = 2 * q + h
                            need(act, m["mm"], at(0) * PAIRS + pair + 1)
                            if h == 0:
                                stored.done(act, c, 0, UNITS, q - UNITS)
                            nc.scalar.activation(raw[:, q, h * 2 * BLK:(h + 1) * 2 * BLK],
                                                 pp[(u * PAIRS + pair) % 4][:, :, :].rearrange("p a t -> p (a t)"),
                                                 ACT.Copy).then_inc(m["out"], 1)
                        if q == 0:
                            quantise_next()
                pipeline(act, tick, NB, U, before=1)

            @block.tensor
            def _(pe):
                def tick(c):
                    at, live, u = c.at, c.live, c.u
                    need(pe, m["al"], at(1))
                    for pair in range(PAIRS):
                        need(pe, m["out"], at(0) * PAIRS + pair - 3)
                        bank = pp[(u * PAIRS + pair) % 4]
                        for h in range(2):
                            f = (2 * pair + h) * P
                            todo = [(w, a, c) for c in range(DC) for w, a in ((0, ah), (0, al), (1, ah))]
                            for q, (w, a, c) in enumerate(todo):
                                mm = nc.tensor.matmul(bank[:, h, :], wt[w][:, c, f:f + P], a[:, u % 2, :, c, :],
                                                      start=(q == 0), stop=(q == len(todo) - 1))
                        mm.then_inc(m["mm"], 1)
                pipeline(pe, tick, NB, U)


def product_peak(nc, keep, gate_q, up_d, NB):
    g = keep["g"]
    N, U = NB * UNITS, 4
    uv = up_d.rearrange("b q p d -> (b q) p d")
    with Scope(nc, "pp") as s:
        gq, ui = s.sb("gq", [P, 4, UE], I16), s.sb("ui", [P, 4, UE], F32)
        sig, sq = s.sb("sig", [P, 2, UE], F32), s.sb("sq", [P, UE], U16)
        gp = s.sb("gp", [P, 4, UE], F32)
        ga, ua = s.sb("ga", [P, 2, UE], I16), s.sb("ua", [P, 2, UE], I16)
        junk = s.sb("junk", [P, UE], F32)
        col = s.sb("col", [P, 4], F32)
        gin, uin = Transfers(s, "gin", 4), Transfers(s, "uin", 4)
        m = s.sems("g_red g_all u_red u_all dve scales sig sq gp ga ua prod col")
        pg, pg_v, pg_p = whole_peak(nc, s, m, "g", keep["gated_peak"][:, :])
        pu, pu_v, pu_p = whole_peak(nc, s, m, "u", keep["up_peak"][:, :])

        with nc.Block() as block:
            @block.sync
            def _(sp):
                def tick(c):
                    at, live, u = c.at, c.live, c.u
                    if live(4):
                        need(sp, m["gp"], at(1))
                        sp.dma_start(gq[:, u, :], gate_q[bass.ds(at(4), 1)].rearrange("a p d -> p (a d)")).then_inc(gin.of(c, 4), 16)
                    if live(3):
                        need(sp, m["ua"], at(0))
                        sp.dma_start(ui[:, (u + 3) % 4, :], uv[bass.ds(at(3), 1)].rearrange("a p d -> p (a d)")).then_inc(uin.of(c, 3), 16)
                pipeline(sp, tick, N, U, before=4)

            @block.gpsimd
            def _(pool):
                pg_p(pool)
                pu_p(pool)

            @block.scalar
            def _(act):
                def tick(c):
                    at, live, u = c.at, c.live, c.u
                    if live(2):
                        gin.done(act, c, 2)
                        need(act, m["sq"], at(1))
                        nc.scalar.activation(sig[:, u % 2, :], gq[:, (u + 2) % 4, :], ACT.Sigmoid, scale=g[:, 4:5]).then_inc(m["sig"], 1)
                    if live(0):
                        if c.first():
                            act.wait_ge(m["scales"], 1)
                        need(act, m["gp"], at(1))
                        need(act, m["prod"], at(-1))
                        nc.scalar.activation(ga[:, u % 2, :], gp[:, u, :], ACT.Abs, scale=g[:, 7:8]).then_inc(m["ga"], 1)
                        uin.done(act, c)
                        nc.scalar.activation(ua[:, u % 2, :], ui[:, u, :], ACT.Abs, scale=g[:, 10:11]).then_inc(m["ua"], 1)
                pipeline(act, tick, N, U, before=2)

            @block.vector
            def _(dve):
                link = chain(dve, m["dve"])
                pg_v(dve)
                pu_v(dve)
                link(nc.vector.tensor_scalar(g[:, 6:7], g[:, 4:5], 1.0 / 65536.0, None, ALU.mult))
                dve.wait_ge(m["g_all"], 1)
                quantiser(nc, link, g[:, 8:9], g[:, 7:8], pg[:, :], g[:, 6:7])
                dve.wait_ge(m["u_all"], 1)
                quantiser(nc, link, g[:, 9:10], g[:, 10:11], pu[:, :], g[:, 3:4])
                nc.vector.tensor_tensor(g[:, 11:12], g[:, 8:9], g[:, 9:10], ALU.mult).then_inc(m["scales"], 1)

                def tick(c):
                    at, live, u = c.at, c.live, c.u
                    if live(2):
                        need(dve, m["sig"], at(3))
                        need(dve, m["gp"], at(2))
                        nc.vector.tensor_scalar(sq[:, :], sig[:, u % 2, :], 65536.0, 65535.0, ALU.mult, ALU.min).then_inc(m["sq"], 1)
                        need(dve, m["sq"], at(3))
                        need(dve, m["ga"], at(-1))
                        nc.vector.tensor_tensor(gp[:, (u + 2) % 4, :], gq[:, (u + 2) % 4, :], sq[:, :], ALU.mult).then_inc(m["gp"], 1)
                    if live(0):
                        need(dve, m["ua"], at(1))
                        need(dve, m["ga"], at(1))
                        need(dve, m["col"], at(-1))
                    if live(-1):
                        need(dve, m["prod"], at(0))
                        nc.vector.tensor_copy(keep["o_peak"][:, bass.ds(at(-1), 1)], col[:, (u - 1) % 4:(u - 1) % 4 + 1]).then_inc(m["col"], 1)
                    if live(0):
                        nc.vector.tensor_tensor_reduce(out=junk[:, :], in0=ga[:, u % 2, :], in1=ua[:, u % 2, :], scale=1.0,
                                                       scalar=0.0, op0=ALU.mult, op1=ALU.max,
                                                       accum_out=col[:, u % 4:u % 4 + 1]).then_inc(m["prod"], 1)
                pipeline(dve, tick, N, U, before=2, after=1)


def feed_out(nc, keep, gate_q, up_d, x1_d, out, NB):
    g = keep["g"]
    wt = keep["down"]
    U = 2
    out_v = out.rearrange("(b n p) d -> b p n d", p=P, n=SUB)
    x1_v = x1_d.rearrange("(b n) p d -> b p n d", n=SUB)
    up_u = up_d.rearrange("b q p d -> (b q) p d")
    with Scope(nc, "fo") as s:
        gi, ui = s.sb("gi", [P, 3, UE], I16), s.sb("ui", [P, 3, UE], F32)
        sig, sq = s.sb("sig", [P, 2, UE], F32), s.sb("sq", [P, UE], U16)
        gp = s.sb("gp", [P, 2, UE], F32)
        gq, uq = (s.sb(n, [P, 2, UE], I16) for n in ("gq", "uq"))
        oq = s.sb("oq", [P, UE], I16)
        o = s.sb("o", [P, UE], F32)
        oh, ol = (s.sb(n, [P, 2, FC, BLK], F16) for n in ("oh", "ol"))
        xb = s.sb("xb", [P, 2, SUB, D], F32)
        py = [s.ps(f"py{i}", [P, D]) for i in range(8)]
        gin, uin = Transfers(s, "gin", 3), Transfers(s, "uin", 3)
        x_in, stored = Transfers(s, "x_in", 2), Transfers(s, "stored", 2)
        m = s.sems("o_red o_all dve scales sig sq gp gq uq o oq oh ol mm y")
        po, po_v, po_p = whole_peak(nc, s, m, "o", keep["o_peak"][:, :])

        with nc.Block() as block:
            @block.sync
            def _(sp):
                def tick(c):
                    at, live, u = c.at, c.live, c.u
                    for q in range(UNITS):
                        n = at(0) * UNITS + q
                        if c.live_unit(UNITS, q + 6):
                            need(sp, m["gp"], n + 4)
                            sp.dma_start(gi[:, q, :], gate_q[bass.ds(n + 6, 1)].rearrange("a p d -> p (a d)")).then_inc(gin.of(c, 0, UNITS, q + 6), 16)
                        if c.live_unit(UNITS, q + 5):
                            need(sp, m["uq"], n + 3)
                            sp.dma_start(ui[:, (q + 5) % 3, :], up_u[bass.ds(n + 5, 1)].rearrange("a p d -> p (a d)")).then_inc(uin.of(c, 0, UNITS, q + 5), 16)
                    if live(0):
                        stored.done(sp, c, -2)
                        sp.dma_start(xb[:, u % 2], x1_v[bass.ds(at(0), 1)].rearrange("a p n d -> p (a n) d")).then_inc(x_in.of(c), 16)
                    if live(-1):
                        need(sp, m["y"], at(0) * SUB)
                        sp.dma_start(out_v[bass.ds(at(-1), 1)].rearrange("a p n d -> p (a n) d"), xb[:, (u + 1) % 2]).then_inc(stored.of(c, -1), 16)
                pipeline(sp, tick, NB, U, before=2, after=1)
                stored.all_done(sp, NB)

            @block.gpsimd
            def _(pool):
                po_p(pool)

            @block.scalar
            def _(act):
                def tick(c):
                    at, live, u = c.at, c.live, c.u
                    for q in range(UNITS):
                        n = at(0) * UNITS + q
                        if c.live_unit(UNITS, q + 5):
                            gin.done(act, c, 0, UNITS, q + 5)
                            need(act, m["sq"], n + 4)
                            nc.scalar.activation(sig[:, (u * UNITS + q + 5) % 2, :], gi[:, (q + 5) % 3, :], ACT.Sigmoid,
                                                 scale=g[:, 4:5]).then_inc(m["sig"], 1)
                        if c.live_unit(UNITS, q + 4):
                            k = (u * UNITS + q) % 2
                            need(act, m["gp"], n + 5)
                            need(act, m["o"], n + 3)
                            nc.scalar.activation(gq[:, k, :], gp[:, k, :], ACT.Copy, scale=g[:, 7:8]).then_inc(m["gq"], 1)
                            uin.done(act, c, 0, UNITS, q + 4)
                            nc.scalar.activation(uq[:, k, :], ui[:, (q + 4) % 3, :], ACT.Copy, scale=g[:, 10:11]).then_inc(m["uq"], 1)
                        if c.live_unit(UNITS, q + 3):
                            if c.first(0, UNITS, q + 3):
                                act.wait_ge(m["scales"], 1)
                            need(act, m["o"], n + 4)
                            need(act, m["ol"], n + 3)
                            nc.scalar.activation(oq[:, :], o[:, :], ACT.Copy, scale=g[:, 13:14]).then_inc(m["oq"], 1)
                pipeline(act, tick, NB, U, before=2)

            @block.vector
            def _(dve):
                link = chain(dve, m["dve"])
                po_v(dve)
                dve.wait_ge(m["o_all"], 1)
                quantiser(nc, link, g[:, 12:13], g[:, 13:14], po[:, :], g[:, 11:12])
                nc.vector.tensor_tensor(g[:, 14:15], g[:, 12:13], keep["alpha"][:, 6:7], ALU.mult).then_inc(m["scales"], 1)
                dve.wait_ge(m["scales"], 1)

                def tick(c):
                    at, live, u = c.at, c.live, c.u

                    def sum_out(t):
                        need(dve, m["mm"], at(-1) * SUB + t + 1)
                        if t == 0:
                            x_in.done(dve, c, -1)
                        nc.vector.scalar_tensor_tensor(out=xb[:, (u - 1) % 2, t, :], in0=py[((u - 1) * SUB + t) % 8][:, :],
                                                       scalar=g[:, 14:15], in1=xb[:, (u - 1) % 2, t, :],
                                                       op0=ALU.mult, op1=ALU.add).then_inc(m["y"], 1)
                    for q in range(UNITS):
                        n = at(0) * UNITS + q
                        if c.live_unit(UNITS, q + 5):
                            k = (u * UNITS + q + 5) % 2
                            need(dve, m["sig"], n + 6)
                            need(dve, m["gp"], n + 5)
                            nc.vector.tensor_scalar(sq[:, :], sig[:, k, :], 65536.0, 65535.0, ALU.mult, ALU.min).then_inc(m["sq"], 1)
                            need(dve, m["sq"], n + 6)
                            need(dve, m["gq"], n + 4)
                            nc.vector.tensor_tensor(gp[:, k, :], gi[:, (q + 5) % 3, :], sq[:, :], ALU.mult).then_inc(m["gp"], 1)
                        if c.live_unit(UNITS, q + 3):
                            f = (q + 3) % UNITS
                            b = (u + (q + 3) // UNITS) % 2
                            hi = oh[:, b, f * UN:(f + 1) * UN, :].rearrange("p f t -> p (f t)")
                            lo = ol[:, b, f * UN:(f + 1) * UN, :].rearrange("p f t -> p (f t)")
                            need(dve, m["oq"], n + 4)
                            if q == 0:
                                need(dve, m["mm"], at(0) * SUB)
                            nc.vector.tensor_copy(hi, oq[:, :]).then_inc(m["oh"], 1)
                        if c.live_unit(UNITS, q + 4):
                            k = (u * UNITS + q) % 2
                            need(dve, m["gq"], n + 5)
                            need(dve, m["uq"], n + 5)
                            need(dve, m["oq"], n + 4)
                            nc.vector.tensor_tensor(o[:, :], gq[:, k, :], uq[:, k, :], ALU.mult).then_inc(m["o"], 1)
                        if c.live_unit(UNITS, q + 3):
                            need(dve, m["oh"], n + 4)
                            nc.vector.tensor_tensor(lo, oq[:, :], hi, ALU.subtract).then_inc(m["ol"], 1)
                        if live(-1):
                            sum_out(q)
                    if live(-1):
                        sum_out(SUB - 1)
                pipeline(dve, tick, NB, U, before=2, after=1)

            @block.tensor
            def _(pe):
                def tick(c):
                    at, live, u = c.at, c.live, c.u
                    for q in range(UNITS):
                        need(pe, m["ol"], at(0) * UNITS + q + 1)
                        for t in range(SUB):
                            if q == 0:
                                need(pe, m["y"], at(0) * SUB + t - 7)
                            todo = [(a, w, f) for f in range(q * UN, (q + 1) * UN) for a, w in ((oh, 0), (oh, 1), (ol, 0))]
                            for i, (a, w, f) in enumerate(todo):
                                mm = nc.tensor.matmul(py[(u * SUB + t) % 8][:, :], a[:, u % 2, f, t * P:(t + 1) * P],
                                                      wt[w][:, f, :], start=(q == 0 and i == 0),
                                                      stop=(q == UNITS - 1 and i == len(todo) - 1))
                            if q == UNITS - 1:
                                mm.then_inc(m["mm"], 1)
                pipeline(pe, tick, NB, U)


def identity(nc, keep):
    with Scope(nc, "id") as s:
        made = s.sem("made")
        with nc.Block() as block:
            @block.gpsimd
            def _(pool):
                nc.gpsimd.memset(keep["ident32"][:, :], 0.0).then_inc(made, 1)
                pool.wait_ge(made, 1)
                nc.gpsimd.affine_select(out=keep["ident32"][:, :], in_=keep["ident32"][:, :], compare_op=ALU.not_equal,
                                        fill=1.0, base=0, pattern=[[-1, P]], channel_multiplier=1).then_inc(made, 1)
                pool.wait_ge(made, 2)
                nc.gpsimd.tensor_copy(keep["ident16"][:, :], keep["ident32"][:, :]).then_inc(made, 1)
                nc.gpsimd.memset(keep["neg16"][:, :], 0.0).then_inc(made, 1)
                pool.wait_ge(made, 4)
                nc.gpsimd.affine_select(out=keep["neg16"][:, :], in_=keep["neg16"][:, :], compare_op=ALU.not_equal,
                                        fill=-1.0, base=0, pattern=[[-1, P]], channel_multiplier=1).then_inc(made, 1)
                pool.wait_ge(made, 5)


def build(nc, x, ctx_t, idx_t, wq_t, wkv_t, wo_t, gate_n, up_n, down_n, out, B, LKV):
    T = x.shape[0]
    NT, NB = T // P, T // BLK
    table = nc.dram_tensor("kv_table", [B * (LKV + 6), 2 * D], F32).ap()
    x1_d = nc.dram_tensor("x1_scratch", [NT, P, D], F32).ap()
    hT_d = nc.dram_tensor("hT_scratch", [NT, P, D], F32).ap()
    gate_d = nc.dram_tensor("gate_scratch", [NB, UNITS, P, UE], F32).ap()
    up_d = nc.dram_tensor("up_scratch", [NB, UNITS, P, UE], F32).ap()
    gate_q = nc.dram_tensor("gate_integers", [NB * UNITS, P + 1, UE], I16).ap()[:, 0:P, :]
    U3 = NB * UNITS
    with Scope(nc, "kept") as s:
        keep = {
            "down": [s.sb(f"down{i}", [P, FC, D], F16) for i in range(2)],
            "alpha": s.sb("alpha", [P, 12], F32),
            "g": s.sb("g", [P, 16], F32),
            "h_peak": s.sb("h_peak", [P, NT], F32), "gate_peak": s.sb("gate_peak", [P, U3], F32),
            "up_peak": s.sb("up_peak", [P, U3], F32), "gated_peak": s.sb("gated_peak", [P, U3], F32),
            "o_peak": s.sb("o_peak", [P, U3], F32),
        }
        with Scope(nc, "kept") as s_up:
            keep["up"] = [s_up.sb(f"up{i}", [P, DC, F], F16) for i in range(2)]
            with Scope(nc, "kept") as s_gate:
                keep["gate"] = [s_gate.sb(f"gate{i}", [P, DC, F], F16) for i in range(2)]
                with Scope(nc, "kept") as s_att:
                    for n in ("wq", "wo"):
                        keep[n] = [s_att.sb(f"{n}{i}", [P, DC, D], F16) for i in range(2)]
                    for n, shape, dt in (("ident32", [P, P], F32), ("ident16", [P, P], F16), ("neg16", [P, P], F16), ("rows", [P, NT], I32),
                                         ("mask", [P, NT, W], F32), ("rstd", [P, NT], F32), ("shift", [P, NT], F32)):
                        keep[n] = s_att.sb(n, shape, dt)
                    identity(nc, keep)
                    with Scope(nc, "early") as s_in:
                        early = {n: s_in.sb(f"f_{n}", list(src.shape), dt) for n, src, dt in (
                            ("wkv", wkv_t, F32), ("ctx", ctx_t, F32), ("ids", idx_t, I32))}
                        early["loads"] = list(zip(early.values(), (wkv_t, ctx_t, idx_t)))
                        early["loaded"] = [s_in.sem(f"loaded{i}") for i in range(3)]
                        prepare_quant(nc, keep, early, gate_n, up_n, down_n)
                        prepare_dense(nc, keep, early, x, wq_t, wo_t, table, B, LKV)
                    attention(nc, keep, x, table, x1_d, hT_d, B)
                feed_in(nc, keep, hT_d, gate_d, NB)
            feed_in(nc, keep, hT_d, up_d, NB, gate_d, gate_q)
        product_peak(nc, keep, gate_q, up_d, NB)
        feed_out(nc, keep, gate_q, up_d, x1_d, out, NB)


def kernel(x, ctx_1024, itok_BxS_0_511, L0_xattn_Wq, L0_xattn_Wkv, L0_xattn_Wo, L0_ffn_w_gate, L0_ffn_w_up,
           L0_ffn_w_down):
    import numpy as np
    import concourse.bacc as bacc
    from concourse import mybir
    from concourse.bass_utils import run_bass_kernel_spmd

    B, LQ, _ = x.shape
    LKV = ctx_1024.shape[1]

    def contraction_first(w):
        w = np.asarray(w)
        return np.ascontiguousarray(w.T.reshape(DC, P, -1).transpose(1, 0, 2)).reshape(P, -1)

    def by_partition(w):
        w = np.asarray(w)
        return np.ascontiguousarray(w.reshape(-1, P, w.shape[1]).transpose(1, 0, 2)).reshape(P, -1)

    arrays = {
        "x": np.ascontiguousarray(np.asarray(x).reshape(B * LQ, D)),
        "ctx_t": contraction_first(np.asarray(ctx_1024).reshape(B * LKV, D)),
        "idx_t": np.ascontiguousarray(np.asarray(itok_BxS_0_511).reshape(-1, P).T),
        "wq_t": contraction_first(L0_xattn_Wq), "wkv_t": contraction_first(L0_xattn_Wkv),
        "wo_t": contraction_first(L0_xattn_Wo), "gate_n": by_partition(L0_ffn_w_gate),
        "up_n": by_partition(L0_ffn_w_up), "down_n": by_partition(L0_ffn_w_down),
    }
    nc = bacc.Bacc("TRN2", target_bir_lowering=False, num_devices=1)
    args = [nc.dram_tensor(f"in_{n}", a.shape, mybir.dt.from_np(a.dtype), kind="ExternalInput").ap()
            for n, a in arrays.items()]
    out = nc.dram_tensor("out", (B * LQ, D), mybir.dt.float32, kind="ExternalOutput").ap()
    build(nc, *args, out, B, LKV)
    r = run_bass_kernel_spmd(nc, [{f"in_{n}": a for n, a in arrays.items()}], core_ids=[0])
    return r.results[0]["out"].reshape(B, LQ, D)
```
